# Optimizing a Trainium2 kernel written in Bass

```python
import numpy as np
import jax
import jax.numpy as jnp

def _softmax(x, axis=-1):
    return jax.nn.softmax(x, axis=axis)

def _gelu(x):
    return jax.nn.gelu(x, approximate=True)

def _silu(x):
    return jax.nn.silu(x)

def _sigmoid(x):
    return jax.nn.sigmoid(x)

def _layernorm(x, axis=-1, eps=1e-05):
    m = jnp.mean(x, axis=axis, keepdims=True)
    v = jnp.var(x, axis=axis, keepdims=True)
    return (x - m) / jnp.sqrt(v + eps)

def _scatter_add(tgt, idx, src, axis=0):
    return tgt.at[idx].add(src)

def _segment_sum(src, seg, n):
    return jax.ops.segment_sum(src, seg, n)
kernel_name = 'mk_gnn_preln_d2_gnn_r8_329982'

def setup_inputs(seed: int=0):
    np.random.seed(seed)
    _w = jnp.asarray

    def _rec_inputs():
        import jax
        import jax.numpy as jnp
        _gk = jax.random.key(seed)
        x = -0.000202 + 1 * jax.random.normal(jax.random.fold_in(_gk, 1), (6250, 128), jnp.float32)
        _s = jax.random.randint(jax.random.fold_in(_gk, 2), (100000,), 0, 6250, jnp.int32)
        _d = jax.random.randint(jax.random.fold_in(_gk, 3), (100000,), 0, 6250, jnp.int32)
        _loop = jnp.arange(6250, dtype=jnp.int32)
        src = jnp.concatenate([_s, _d, _loop])
        dst = jnp.concatenate([_d, _s, _loop])
        _o = jnp.argsort(dst, stable=True)
        src = src[_o]
        dst = dst[_o]
        edge_attr_128 = 2.93046e-05 + 1.00006 * jax.random.normal(jax.random.fold_in(_gk, 11), (206250, 128), jnp.float32)
        edge_attr_128_n2 = 2.93046e-05 + 1.00006 * jax.random.normal(jax.random.fold_in(_gk, 12), (206250, 128), jnp.float32)
        return (x, src, dst, edge_attr_128, edge_attr_128_n2)
    x, src, dst, edge_attr_128, edge_attr_128_n2 = _rec_inputs()

    def _L0_gnn_setup():
        import jax, jax.numpy as jnp
        import numpy as np
        N = 6250
        E = 100000
        D = 128
        LN_EPS = 1e-05
        key = jax.random.key(seed)
        ks = jax.random.split(key, 6)
        x = jax.random.normal(ks[0], (N, D), dtype=jnp.float32)
        edge_index = jax.random.randint(ks[1], (2, E), 0, N, dtype=jnp.int64)
        W_lin = jax.random.normal(ks[2], (D, D), dtype=jnp.float32) / np.sqrt(D).astype(np.float32)
        W_gcn = jax.random.normal(ks[3], (D, D), dtype=jnp.float32) / np.sqrt(D).astype(np.float32)
        b_gcn = jnp.zeros((D,), dtype=jnp.float32)
        gamma = jnp.ones((D,), dtype=jnp.float32)
        beta = jnp.zeros((D,), dtype=jnp.float32)
        return {'x': x, 'edge_index': edge_index, 'W_lin': W_lin, 'W_gcn': W_gcn, 'b_gcn': b_gcn, 'gamma': gamma, 'beta': beta}
    _L0_gnn_all = _L0_gnn_setup()
    _L0_gnn_in = {k: v for k, v in _L0_gnn_all.items() if k in ('W_lin', 'W_gcn', 'b_gcn', 'gamma', 'beta')}
    del _L0_gnn_all

    def _L1_gnn_setup():
        import jax, jax.numpy as jnp
        import numpy as np
        N, E, DIM, HEADS = (1250, 80000, 128, 4)
        key = jax.random.key(seed)
        ks = jax.random.split(key, 13)
        s = 1.0 / np.sqrt(DIM)
        inp = {'q_nodes': jax.random.normal(ks[0], (N, DIM), jnp.float32), 'k_edges': jax.random.normal(ks[1], (E, DIM), jnp.float32), 'v_edges': jax.random.normal(ks[2], (E, DIM), jnp.float32), 'Wq': jax.random.normal(ks[3], (DIM, DIM), jnp.float32) * s, 'bq': jax.random.normal(ks[4], (DIM,), jnp.float32) * s, 'Wk': jax.random.normal(ks[5], (DIM, DIM), jnp.float32) * s, 'bk': jax.random.normal(ks[6], (DIM,), jnp.float32) * s, 'Wv': jax.random.normal(ks[7], (DIM, DIM), jnp.float32) * s, 'bv': jax.random.normal(ks[8], (DIM,), jnp.float32) * s, 'Wo': jax.random.normal(ks[9], (DIM, DIM), jnp.float32) * s, 'bo': jax.random.normal(ks[10], (DIM,), jnp.float32) * s, 'edge_index': jax.random.randint(ks[11], (2, E), 0, N, jnp.int64)}
        return inp
    _L1_gnn_all = _L1_gnn_setup()
    _L1_gnn_in = {k: v for k, v in _L1_gnn_all.items() if k in ('Wq', 'bq', 'Wk', 'bk', 'Wv', 'bv', 'Wo', 'bo')}
    del _L1_gnn_all
    return {'x': x, 'src': src, 'dst': dst, 'edge_attr_128': edge_attr_128, 'edge_attr_128_n2': edge_attr_128_n2, 'L0_gnn_W_lin': _L0_gnn_in['W_lin'], 'L0_gnn_W_gcn': _L0_gnn_in['W_gcn'], 'L0_gnn_b_gcn': _L0_gnn_in['b_gcn'], 'L0_gnn_gamma': _L0_gnn_in['gamma'], 'L0_gnn_beta': _L0_gnn_in['beta'], 'L1_gnn_Wq': _L1_gnn_in['Wq'], 'L1_gnn_bq': _L1_gnn_in['bq'], 'L1_gnn_Wk': _L1_gnn_in['Wk'], 'L1_gnn_bk': _L1_gnn_in['bk'], 'L1_gnn_Wv': _L1_gnn_in['Wv'], 'L1_gnn_bv': _L1_gnn_in['bv'], 'L1_gnn_Wo': _L1_gnn_in['Wo'], 'L1_gnn_bo': _L1_gnn_in['bo']}

def reference(x, src, dst, edge_attr_128, edge_attr_128_n2, L0_gnn_W_lin, L0_gnn_W_gcn, L0_gnn_b_gcn, L0_gnn_gamma, L0_gnn_beta, L1_gnn_Wq, L1_gnn_bq, L1_gnn_Wk, L1_gnn_bk, L1_gnn_Wv, L1_gnn_bv, L1_gnn_Wo, L1_gnn_bo):
    import jax
    import jax.numpy as jnp

    def _L0_gnn_ref(x, edge_index, W_lin, W_gcn, b_gcn, gamma, beta):
        import jax, jax.numpy as jnp
        import numpy as np
        N = 6250
        E = 100000
        D = 128
        LN_EPS = 1e-05
        n = x.shape[0]
        h = x @ W_lin.T if False else x @ W_lin
        h = h @ W_gcn
        loops = jnp.arange(n, dtype=edge_index.dtype)
        src = jnp.concatenate([edge_index[0], loops])
        dst = jnp.concatenate([edge_index[1], loops])
        deg = jax.ops.segment_sum(jnp.ones_like(dst, dtype=h.dtype), dst, num_segments=n)
        dinv = jnp.where(deg > 0, jax.lax.rsqrt(jnp.maximum(deg, 1e-12)), 0.0)
        norm = dinv[src] * dinv[dst]
        msg = h[src] * norm[:, None]
        out = jax.ops.segment_sum(msg, dst, num_segments=n) + b_gcn
        mu = jnp.mean(out, axis=-1, keepdims=True)
        var = jnp.mean(jnp.square(out - mu), axis=-1, keepdims=True)
        y = (out - mu) * jax.lax.rsqrt(var + LN_EPS) * gamma + beta
        return jax.nn.relu(y)

    def _L1_gnn_ref(q_nodes, k_edges, v_edges, Wq, bq, Wk, bk, Wv, bv, Wo, bo, edge_index):
        import jax, jax.numpy as jnp
        import numpy as np
        N, E, DIM, HEADS = (1250, 80000, 128, 4)
        n, dim = q_nodes.shape
        e = k_edges.shape[0]
        heads = HEADS
        d_head = dim // heads
        scale = d_head ** (-0.5)
        dst = edge_index[0]
        q = (q_nodes @ Wq + bq).reshape(n, heads, d_head)
        k = (k_edges @ Wk + bk).reshape(e, heads, d_head)
        v = (v_edges @ Wv + bv).reshape(e, heads, d_head)
        score = jnp.einsum('ehd,ehd->eh', q[dst], k) * scale
        seg_max = jax.ops.segment_max(score, dst, num_segments=n)
        ex = jnp.exp(score - seg_max[dst])
        denom = jax.ops.segment_sum(ex, dst, num_segments=n)
        attn = ex / denom[dst]
        weighted = (v * attn[..., None]).reshape(e, dim)
        agg = jax.ops.segment_sum(weighted, dst, num_segments=n)
        return agg @ Wo + bo
    edge_index = jnp.stack([src, dst])
    h = jnp.maximum(_layernorm(x, axis=-1), 0.0)
    x = x + _L0_gnn_ref(h, edge_index, L0_gnn_W_lin, L0_gnn_W_gcn, L0_gnn_b_gcn, L0_gnn_gamma, L0_gnn_beta)
    h = jnp.maximum(_layernorm(x, axis=-1), 0.0)
    x = x + _L1_gnn_ref(h, edge_attr_128, edge_attr_128_n2, L1_gnn_Wq, L1_gnn_bq, L1_gnn_Wk, L1_gnn_bk, L1_gnn_Wv, L1_gnn_bv, L1_gnn_Wo, L1_gnn_bo, edge_index)
    return x

_drawn_inputs = setup_inputs


def setup_inputs(seed=0):
    import zlib

    import numpy as np

    out = dict(_drawn_inputs(seed))
    spreads = {'L0_gnn_b_gcn': (0.0, 0.1), 'L0_gnn_gamma': (1.0, 0.2), 'L0_gnn_beta': (0.0, 0.1)}
    factors = {'L1_gnn_bq': 3.803, 'L1_gnn_bk': 8.0}
    for name, (base, spread) in spreads.items():
        noise = np.random.default_rng([zlib.crc32(name.encode()), seed]).standard_normal(out[name].shape)
        drawn = base * np.exp(spread * noise) if base else spread * noise
        out[name] = jnp.asarray(drawn.astype(out[name].dtype))
    for name, factor in factors.items():
        out[name] = (out[name] * factor).astype(out[name].dtype)
    return out
```

```python
from contextlib import ExitStack

import concourse.bass as bass
from concourse import mybir

F32 = mybir.dt.float32
I32 = mybir.dt.int32
BF16 = mybir.dt.bfloat16
ALU = mybir.AluOpType
ACT = mybir.ActivationFunctionType
AX_X = mybir.AxisListType.X

P = 128
D = 128
N = 6250
E = 206250
HEADS = 4
DH = D // HEADS
SCALE = float(DH) ** -0.5
EPS = 1e-5

TILES = -(-N // P)
NT = TILES + TILES % 2
SN = P // HEADS
PARTS = P // SN
STILES = -(-N // SN)
COLS = 1616
SC = 8
GC = 4
GE = GC * P
RING = 4
SGC = 3
SGE = SGC * P
SRING = 6
VW = D + 1


def groups(tiles, slots, ring):
    n = -(-(E + tiles * (slots - 1)) // slots)
    return n + -n % ring


NGD = groups(TILES, GE, RING)
NGS = groups(STILES, SGE, SRING)
USUAL = STILES * -(-E // (STILES * SGE))
USUAL += USUAL // 50 + -(USUAL + USUAL // 50) % SRING
PAD_KEY = P * P - 1
BIG = 2.0 ** 100
FLOOR = -1.0e29
FULL = E // COLS
REST = E - FULL * COLS
EDGES = P * COLS
SORTED_AT = EDGES + GE
NEXT_OUT_OF_ORDER = 63
PLACED_PER_ROUND = 2
BANKS = 4
BANK_COLS = COLS // BANKS
LOADS_W = 13
assert EDGES >= E and COLS % (2 * SC) == 0 and PAD_KEY // P >= TILES and COLS % BANKS == 0 and BANK_COLS <= 512
assert STILES % PLACED_PER_ROUND == 0 and STILES // PLACED_PER_ROUND <= NGD // RING and STILES == PARTS * TILES


def need(eng, sem, count):
    if not isinstance(count, int) or count > 0:
        eng.wait_ge(sem, count)


def apart(m, eng, sem, count):
    if not isinstance(count, int) or count > 0:
        eng.wait_ge(sem, count)
        eng.sem_inc(m["held"], 1)


def steps(eng, body, first, last, unroll):
    for u in range(unroll):
        body(first * unroll + u, u, first)
    with eng.Fori(first + 1, last - 1) as r:
        for u in range(unroll):
            body(r * unroll + u, u, r)
    for u in range(unroll):
        body((last - 1) * unroll + u, u, last - 1)


def rounds(eng, body, first, last, unroll):
    if first == 0:
        for u in range(unroll):
            body(u, u, 0)
    with eng.Fori(max(first, 1), last) as r:
        for u in range(unroll):
            body(r * unroll + u, u, r)


def zero(i):
    return isinstance(i, int) and i == 0


class Chain:

    def __init__(self, eng, sem, start=0):
        self.eng, self.sem, self.n = eng, sem, start

    def __call__(self, ins):
        ins.then_inc(self.sem, 1)
        self.n = self.n + 1
        self.eng.wait_ge(self.sem, self.n)


def column(ap, shape):
    return ap.rearrange("p (t a) -> p t a", a=1).to_broadcast(shape)


def row_of(ap, shape):
    return ap.rearrange("p (a d) -> p a d", a=1).to_broadcast(shape)


def node_tiles(ap):
    return ap.rearrange("(t p) d -> p t d", p=P)


def in_partitions(ap):
    return ap.rearrange("(p c) w -> p c w", p=P)



def load(nc, m, sp):
    sp.wait_ge(m["paddings"], 1)
    dst, src = m["keys"]["dst"], m["keys"]["src"]
    for t, k, shift in ((m["raw"]["dst"], dst, 0), (m["next"], dst, 1), (m["raw"]["src"], src, 0)):
        sp.dma_start(t[0:FULL // 16 * 16, :], k[shift:shift + FULL // 16 * 16 * COLS].rearrange("(p j) -> p j", j=COLS)).then_inc(m["keys_loaded"], 16)
        sp.dma_start(t[FULL // 16 * 16:FULL, :], k[shift + FULL // 16 * 16 * COLS:shift + FULL * COLS].rearrange("(p j) -> p j", j=COLS)).then_inc(m["keys_loaded"], 16)
        sp.dma_start(t[FULL:FULL + 1, 0:REST - shift], k[shift + FULL * COLS:E].rearrange("(a j) -> a j", a=1)).then_inc(m["keys_loaded"], 16)
    sp.dma_start(m["xres"][:, 0:N // P, :], node_tiles(m["x"][0:N // P * P, :])).then_inc(m["x_loaded"], 16)
    sp.dma_start(m["xres"][0:N % P, N // P, :], m["x"][N // P * P:N, :]).then_inc(m["x_loaded"], 16)
    for n in ("W_lin", "W_gcn", "Wq", "Wk", "Wv", "Wo"):
        sp.dma_start(m["w"][n][:, :], m["arg"][n]).then_inc(m["w_loaded"], 16)
    for n in ("bq", "bk", "bv"):
        sp.dma_start(m["w"][n][:, :], m["arg"][n].rearrange("(p a) -> p a", a=1)).then_inc(m["w_loaded"], 16)
    for n in ("b_gcn", "gamma", "beta", "bo"):
        sp.dma_start(m["w"][n][:, :], m["arg"][n].rearrange("(a d) -> a d", a=1).to_broadcast([P, D])).then_inc(m["w_loaded"], 16)


def constants(nc, m, pool):
    c = Chain(pool, m["pool_chain"])
    for t in (m["raw"]["dst"], m["next"], m["raw"]["src"]):
        pool.memset(t[:, :], PAD_KEY)
    pool.memset(m["xres"][:, N // P:NT, :], 0.0)
    pool.memset(m["cnt"][:, :], 0.0).then_inc(m["paddings"], 1)
    for t, value in ((m["ones_b"], 1.0), (m["ones"], 1.0)):
        pool.memset(t[:, :], value)
    pool.memset(m["empty"][:, :, 0:1], 0)
    pool.memset(m["empty"][:, :, 1:2], PAD_KEY)
    for t, sign in ((m["iota_d"], 1), (m["iota_s"], 1), (m["iota_n"], 1), (m["iota_t"], 1), (m["minus_t"], -1)):
        pool.iota(t[:, :], [[sign, t.shape[1]]], base=0, channel_multiplier=0, allow_small_or_imprecise_dtypes=True)
    pool.iota(m["iota_h"][:, :], [[0, HEADS], [1, SN]], base=0, channel_multiplier=0, allow_small_or_imprecise_dtypes=True)
    c(pool.memset(m["headmask"][:, :], 1.0))
    c(pool.memset(m["out_b"][:, :], 0.0))
    c(pool.memset(m["ident"][:, :], 0.0))
    c(pool.memset(m["before"][:, :], 1.0))
    pool.affine_select(out=m["ident"][:, :], in_=m["ident"][:, :], compare_op=ALU.not_equal, fill=1.0, base=0,
                       pattern=[[-1, P]], channel_multiplier=1)
    pool.affine_select(out=m["before"][:, :], in_=m["before"][:, :], compare_op=ALU.is_gt, fill=0.0, base=0,
                       pattern=[[1, P]], channel_multiplier=-1)
    c(pool.affine_select(out=m["out_b"][:, :], in_=m["out_b"][:, :], compare_op=ALU.not_equal, fill=-BIG, base=0,
                         pattern=[[-1, P]], channel_multiplier=1))
    c(pool.affine_select(out=m["headmask"][:, :], in_=m["headmask"][:, :], compare_op=ALU.is_ge, fill=0.0, base=0,
                         pattern=[[-DH, HEADS]], channel_multiplier=1))
    pool.affine_select(out=m["headmask"][:, :], in_=m["headmask"][:, :], compare_op=ALU.is_ge, fill=0.0, base=DH - 1,
                       pattern=[[DH, HEADS]], channel_multiplier=-1).then_inc(m["consts"], 1)


def normalise(nc, m, dve, c, src, centred, squares, turn):
    shape = [P, NT, D]
    c(dve.tensor_reduce(m["stat"][:, :], src[:, :, :], AX_X, ALU.add))
    c(dve.tensor_scalar(m["mean"][:, :], m["stat"][:, :], 1.0 / D, None, ALU.mult))
    c(dve.tensor_tensor(centred[:, :, :], src[:, :, :], column(m["mean"][:, :], shape), ALU.subtract))
    c(dve.tensor_tensor(squares[:, :, :], centred[:, :, :], centred[:, :, :], ALU.mult))
    c(dve.tensor_reduce(m["stat"][:, :], squares[:, :, :], AX_X, ALU.add))
    dve.tensor_scalar(m["var"][:, :], m["stat"][:, :], 1.0 / D, EPS, ALU.mult, ALU.add).then_inc(m["sqrt_asked"], 1)
    dve.wait_ge(m["sqrt_done"], turn)
    c(dve.reciprocal(m["rstd"][:, :], m["std"][:, :]))


def square_root(nc, m, act, turn):
    act.wait_ge(m["sqrt_asked"], turn)
    nc.scalar.activation(m["std"][:, :], m["var"][:, :], ACT.Sqrt).then_inc(m["sqrt_done"], 1)


def count_sums(nc, m, pe, cnt, n, counted, total, ready):
    pe.wait_ge(counted, total)
    pe.matmul(m["bank"][0][:, 0:n], m["before"][:, :], cnt[:, 0:n], start=True, stop=True)
    pe.matmul(m["bank"][1][:, 0:n], m["ones"][:, :], cnt[:, 0:n], start=True, stop=True).then_inc(ready, 1)


def tile_groups(m, dve, c, n, gc, ng, ngi, first, end):
    c(dve.tensor_scalar(ng, m["bank"][1][:, 0:n], float(gc * P - 1), None, ALU.add))
    c(dve.tensor_copy(ngi, ng))
    c(dve.tensor_scalar(ngi, ngi, P.bit_length() - 1, None, ALU.arith_shift_right))
    c(dve.tensor_copy(ng, ngi))
    c(dve.tensor_scalar(ng, ng, float(-(-2 ** 13 // gc)), None, ALU.mult))
    c(dve.tensor_copy(ngi, ng))
    c(dve.tensor_scalar(ngi, ngi, 13, None, ALU.arith_shift_right))
    c(dve.tensor_copy(ng, ngi))
    c(dve.memset(first, 0.0))
    c(dve.tensor_tensor_scan(end, ng, first, 0.0, ALU.add, ALU.add))
    c(dve.tensor_tensor(first, end, ng, ALU.subtract))


def first_block(nc, m):
    with nc.Block() as block:
        @block.sync
        def _(sp):
            load(nc, m, sp)
            sp.wait_ge(m["pairs_ready"], 1)
            sp.dma_start(in_partitions(m["table_d"][0:EDGES, :]), m["pairs"][:, :, :]).then_inc(m["pairs_stored"], 16)
            sp.dma_start(in_partitions(m["table_d"][EDGES:EDGES + GE, :]), m["empty"][:, 0:GE // P, :]).then_inc(m["pairs_stored"], 16)
            t3 = in_partitions(m["table_s"][0:NGS * SGE, :])
            for j in range(0, NGS * SGC, EMPTY):
                n = min(EMPTY, NGS * SGC - j)
                sp.dma_start(t3[:, j:j + n, :], m["empty"][:, 0:n, :]).then_inc(m["emptied"], 16)
            sp.wait_ge(m["pairs_stored"], 32)
            sp.wait_ge(m["emptied"], 16 * -(-NGS * SGC // EMPTY))

        @block.gpsimd
        def _(pool):
            constants(nc, m, pool)

        @block.vector
        def _(dve):
            c = Chain(dve, m["dve_chain"])
            dve.wait_ge(m["consts"], 1)
            dve.wait_ge(m["w_loaded"], 16 * LOADS_W)
            c(dve.tensor_scalar(m["qscale"][:, :], m["headmask"][:, :], SCALE, None, ALU.mult))
            c(dve.tensor_scalar(m["qbias"][:, :], m["qscale"][:, :], m["w"]["bq"][:, 0:1], None, ALU.mult))
            for h in range(HEADS):
                last = dve.tensor_scalar(m["wo_heads"][:, h, :], m["w"]["Wo"][:, :], m["headmask"][:, h:h + 1], None, ALU.mult)
            last.then_inc(m["wo_masked"], 1)
            dve.wait_ge(m["wo_masked"], 1)
            dve.wait_ge(m["x_loaded"], 32)
            normalise(nc, m, dve, c, m["xres"], m["work"], m["acc"], 1)

            def normal(i, u, r):
                need(dve, m["h_transposed"], i - 1)
                dve.tensor_scalar(m["hs"][:, u, :], m["work"][:, bass.ds(i, 1), :], m["rstd"][:, bass.ds(i, 1)], 0.0, ALU.mult,
                                  ALU.max).then_inc(m["h_ready"], 1)
            rounds(dve, normal, 0, NT // 2, 2)
            dve.wait_ge(m["keys_loaded"], 16 * 9)
            one = "p (j a) -> p j a"
            dve.tensor_copy(m["pairs"][:, :, 1:2], m["raw"]["dst"][:, :].rearrange(one, a=1))
            dve.tensor_scalar(m["pairs"][:, :, 0:1], m["raw"]["src"][:, :].rearrange(one, a=1), float(NT * P - 1), None, ALU.min).then_inc(m["pairs_ready"], 1)
            c(dve.tensor_tensor(m["cum"][:, 0, :], m["next"][:, :], m["raw"]["dst"][:, :], ALU.is_lt))
            c(dve.tensor_reduce(m["cnt"][:, NEXT_OUT_OF_ORDER:NEXT_OUT_OF_ORDER + 1], m["cum"][:, 0, :], AX_X, ALU.add))
            mask_i = m["mask"][:, 0, :].bitcast(I32)
            for k, bits, out in (("dst", P.bit_length() - 1, m["square"]), ("src", SN.bit_length() - 1, m["tile_of"])):
                c(dve.tensor_scalar(mask_i, m["raw"][k][:, :], bits, None, ALU.arith_shift_right))
                c(dve.tensor_copy(out[:, :], mask_i))
            with dve.Fori(0, TILES) as b:
                dve.tensor_scalar(m["mask"][:, 0, :], m["square"][:, :], m["iota_t"][:, bass.ds(b, 1)], 0.0, ALU.is_equal, ALU.add,
                                  accum_out=m["cnt"][:, bass.ds(b, 1)]).then_inc(m["counted_d"], 1)
                dve.wait_ge(m["counted_d"], b + 1)
            dve.wait_ge(m["sums_d"], 1)
            n = TILES
            ng, first, end, adj, step = (t[:, 0:n] for t in (m["ng"], m["first_d"], m["end"], m["adj"], m["step"]))
            tile_groups(m, dve, c, n, GC, ng, m["ngi"][:, 0:n], first, end)
            c(dve.tensor_scalar(m["base_d"][:, 0:n], first, float(GE), None, ALU.mult))
            c(dve.tensor_tensor(m["base_d"][:, 0:n], m["base_d"][:, 0:n], m["bank"][0][:, 0:n], ALU.add))
            total = m["bank"][1][:, 0:n]
            c(dve.memset(step, 0.0))
            c(dve.tensor_copy(m["tot"][:, 0:n], total))
            c(dve.tensor_tensor_scan(adj, m["tot"][:, 0:n], step, 0.0, ALU.add, ALU.add))
            c(dve.tensor_tensor(adj, adj, m["tot"][:, 0:n], ALU.subtract))
            c(dve.scalar_tensor_tensor(out=adj, in0=first, scalar=-float(GE), in1=adj, op0=ALU.mult, op1=ALU.add))
            unsorted = m["flags"][:, 0:1]
            c(dve.tensor_copy(m["flags_i"][:, :], m["bank"][1][:, NEXT_OUT_OF_ORDER:NEXT_OUT_OF_ORDER + 1]))
            c(dve.tensor_scalar(unsorted, m["bank"][1][:, NEXT_OUT_OF_ORDER:NEXT_OUT_OF_ORDER + 1], 1.0, None, ALU.min))
            c(dve.tensor_scalar(m["flags"][:, 1:2], unsorted, -1.0, 1.0, ALU.mult, ALU.add))
            c(dve.tensor_scalar(m["flags"][:, 2:3], unsorted, float(SORTED_AT), None, ALU.mult))
            c(dve.tensor_scalar(adj, adj, m["flags"][:, 1:2], m["flags"][:, 2:3], ALU.mult, ALU.add))
            c(dve.tensor_tensor(step[:, 0:n - 1], adj[:, 1:n], adj[:, 0:n - 1], ALU.subtract))
            c(dve.tensor_scalar(m["at_f"][:, :], m["iota_d"][:, :], float(GE), adj[:, 0:1], ALU.mult, ALU.add))
            c(dve.memset(m["tile_d"][:, :], 0.0))
            with dve.Fori(0, TILES - 1) as b:
                dve.tensor_scalar(m["past"][:, 0:NGD], m["iota_d"][:, :], m["end"][:, bass.ds(b, 1)], None, ALU.is_ge).then_inc(m["stepped"], 1)
                dve.wait_ge(m["stepped"], b * 3 + 1)
                dve.tensor_tensor(m["tile_d"][:, :], m["tile_d"][:, :], m["past"][:, 0:NGD], ALU.add).then_inc(m["stepped"], 1)
                dve.scalar_tensor_tensor(out=m["at_f"][:, :], in0=m["past"][:, 0:NGD], scalar=m["step"][:, bass.ds(b, 1)], in1=m["at_f"][:, :],
                                         op0=ALU.mult, op1=ALU.add).then_inc(m["stepped"], 1)
                dve.wait_ge(m["stepped"], b * 3 + 3)
            c(dve.tensor_scalar(m["flags"][:, 2:3], unsorted, float(NGD * GE + SORTED_AT), float(EDGES), ALU.mult, ALU.add))
            c(dve.tensor_scalar(m["at_d"][:, :], m["at_f"][:, :], m["flags"][:, 2:3], None, ALU.min))
            c(dve.tensor_copy(m["tile_di"][:, :], m["tile_d"][:, :]))
            c(dve.tensor_scalar(m["node_d"][:, :], m["tile_d"][:, :], float(P), None, ALU.mult))
            m["chain_at"] = c.n

        @block.scalar
        def _(act):
            act.wait_ge(m["w_transposed"], 1)
            nc.scalar.copy(m["wkT"][:, :], m["bank"][6][:, 0:D])
            nc.scalar.copy(m["wvT"][:, :], m["bank"][7][:, 256:256 + D])
            nc.scalar.copy(m["w_linT"][:, :], m["bank"][7][:, 0:D]).then_inc(m["wT_ready"], 1)
            act.wait_ge(m["w12_summed"], 1)
            nc.scalar.copy(m["w12"][:, :], m["bank"][7][:, 128:128 + D]).then_inc(m["w12_ready"], 1)
            act.wait_ge(m["wvo_summed"], 1)
            nc.scalar.copy(m["wvo"][:, :], m["bank"][0][:, :])
            nc.scalar.copy(m["bvo"][:, :], m["bank"][1][0:1, 0:D]).then_inc(m["wvo_ready"], 1)
            square_root(nc, m, act, 1)

            def copies(i, u, r):
                act.wait_ge(m["h_transposed"], i + 1)
                need(act, m["hw_summed"], i - 1)
                nc.scalar.copy(m["hT"][:, u, :], m["bank"][2 + u][:, 0:P]).then_inc(m["hT_ready"], 1)
                act.wait_ge(m["hw_summed"], i + 1)
                nc.scalar.copy(m["acc"][:, bass.ds(i, 1), :], m["bank"][4 + u][:, 0:D].rearrange("p (a d) -> p a d", a=1)).then_inc(m["hw_read"], 1)
            rounds(act, copies, 0, NT // 2, 2)

        @block.tensor
        def _(pe):
            pe.wait_ge(m["consts"], 1)
            pe.wait_ge(m["w_loaded"], 16 * LOADS_W)
            pe.transpose(m["bank"][6][:, 0:D], m["w"]["Wk"][:, :], m["ident"][:, :])
            pe.transpose(m["bank"][7][:, 256:256 + D], m["w"]["Wv"][:, :], m["ident"][:, :])
            pe.transpose(m["bank"][7][:, 0:D], m["w"]["W_lin"][:, :], m["ident"][:, :]).then_inc(m["w_transposed"], 1)
            pe.wait_ge(m["wT_ready"], 1)
            pe.matmul(m["bank"][7][:, 128:128 + D], m["w_linT"][:, :], m["w"]["W_gcn"][:, :], start=True, stop=True).then_inc(m["w12_summed"], 1)
            pe.wait_ge(m["wo_masked"], 1)
            pe.matmul(m["bank"][0][:, :], m["wvT"][:, :], m["wo_heads"][:, :, :].rearrange("p h d -> p (h d)"), start=True, stop=True)
            pe.matmul(m["bank"][1][0:1, 0:D], m["w"]["bv"][:, 0:1], m["w"]["Wo"][:, :], start=True, stop=True).then_inc(m["wvo_summed"], 1)
            pe.wait_ge(m["w12_ready"], 1)

            def features(i, u, r):
                pe.wait_ge(m["h_ready"], i + 1)
                need(pe, m["hT_ready"], i - 1)
                pe.transpose(m["bank"][2 + u][:, 0:P], m["hs"][:, u, :], m["ident"][:, :]).then_inc(m["h_transposed"], 1)
                pe.wait_ge(m["hT_ready"], i + 1)
                need(pe, m["hw_read"], i - 1)
                pe.matmul(m["bank"][4 + u][:, 0:D], m["hT"][:, u, :], m["w12"][:, :], start=True, stop=True).then_inc(m["hw_summed"], 1)
            rounds(pe, features, 0, NT // 2, 2)
            pe.wait_ge(m["wvo_ready"], 1)
            count_sums(nc, m, pe, m["cnt"], 64, m["counted_d"], TILES, m["sums_d"])



def scatter(nc, m, pool, table, staged, scattered):
    def body(i, u, r):
        apart(m, pool, staged[u], r * 32 + 32)
        for j in range(SC):
            pool.indirect_dma_start(out=table, out_offset=bass.IndirectOffsetOnAxis(ap=m["row_st"][:, u, j:j + 1], axis=0),
                                    in_=m["pair_st"][:, u, j, :], in_offset=None).then_inc(scattered[u], 16)
    rounds(pool, body, 0, COLS // SC // 2, 2)
    for u in range(2):
        pool.wait_ge(scattered[u], COLS // 2 * 16)


def stage(nc, m, sp, staged, scattered):
    def body(i, u, r):
        apart(m, sp, scattered[u], r * (16 * SC))
        sp.dma_start(m["row_st"][:, u, :], m["row"][:, bass.ds(i * SC, SC)]).then_inc(staged[u], 16)
        sp.dma_start(m["pair_st"][:, u, :, :], m["pairs"][:, bass.ds(i * SC, SC), :]).then_inc(staged[u], 16)
    rounds(sp, body, 0, COLS // SC // 2, 2)


def out_of_order(m, eng):
    return eng.value_load(m["flags_i"][0:1, 0:1], min_val=0, max_val=E)


def unsorted_block(nc, m):
    with nc.Block() as block:
        @block.sync
        def _(sp):
            with sp.If(out_of_order(m, sp) > 0):
                t3 = in_partitions(m["table_d"][SORTED_AT:SORTED_AT + NGD * GE, :])
                for j in range(0, NGD * GC, EMPTY):
                    n = min(EMPTY, NGD * GC - j)
                    sp.dma_start(t3[:, j:j + n, :], m["empty"][:, 0:n, :]).then_inc(m["emptied_d"], 16)
                sp.wait_ge(m["emptied_d"], 16 * -(-NGD * GC // EMPTY))
                sp.wait_ge(m["rows_d"], 1)
                stage(nc, m, sp, m["staged_d"], m["scattered_d"])

        @block.gpsimd
        def _(pool):
            with pool.If(out_of_order(m, pool) > 0):
                pool.iota(m["row"][:, :].bitcast(F32), [[1, COLS]], base=SORTED_AT + NGD * GE + 1, channel_multiplier=0,
                          allow_small_or_imprecise_dtypes=True).then_inc(m["junk_d"], 1)
                scatter(nc, m, pool, m["table_d"], m["staged_d"], m["scattered_d"])

        @block.vector
        def _(dve):
            with dve.If(out_of_order(m, dve) > 0):
                c = Chain(dve, m["unsorted_chain"])
                mask, cum, pos = m["mask"][:, 0, :], m["cum"][:, 0, :], m["cum"][:, 1, :]
                dve.wait_ge(m["junk_d"], 1)
                c(dve.tensor_scalar(m["base_d"][:, 0:TILES], m["base_d"][:, 0:TILES], float(SORTED_AT), None, ALU.add))
                c(dve.scalar_tensor_tensor(out=pos, in0=m["square"][:, :], scalar=float(TILES), in1=m["row"][:, :].bitcast(F32),
                                           op0=ALU.is_ge, op1=ALU.mult))
                with dve.Fori(0, TILES) as b:
                    dve.tensor_scalar(mask, m["square"][:, :], m["iota_t"][:, bass.ds(b, 1)], None, ALU.is_equal).then_inc(m["placed_d"], 1)
                    dve.wait_ge(m["placed_d"], b * 4 + 1)
                    dve.tensor_tensor_scan(cum, mask, mask, m["base_d"][:, bass.ds(b, 1)], ALU.add, ALU.max).then_inc(m["placed_d"], 1)
                    dve.wait_ge(m["placed_d"], b * 4 + 2)
                    dve.tensor_tensor(cum, cum, mask, ALU.mult).then_inc(m["placed_d"], 1)
                    dve.wait_ge(m["placed_d"], b * 4 + 3)
                    dve.tensor_tensor(pos, pos, cum, ALU.add).then_inc(m["placed_d"], 1)
                    dve.wait_ge(m["placed_d"], b * 4 + 4)
                dve.tensor_scalar(m["row"][:, :], pos, -1.0, None, ALU.add).then_inc(m["rows_d"], 1)



def layer0_slots(m, eng, i):
    at = eng.value_load(m["at_d"][0:1, bass.ds(i, 1)], min_val=0, max_val=SORTED_AT + (NGD - 1) * GE)
    return in_partitions(m["table_d"][bass.ds(at, GE), :])


def one_hot(dve, out, iota, keys, first_node, shape, compare=ALU.is_equal):
    return dve.scalar_tensor_tensor(out=out, in0=keys.to_broadcast(shape), scalar=first_node, in1=iota.to_broadcast(shape),
                                    op0=ALU.subtract, op1=compare)


def degree_block(nc, m):
    with nc.Block() as block:
        @block.sync
        def _(sp):
            def body(i, u, r):
                slots = layer0_slots(m, sp, i)
                apart(m, sp, m["deg_hot"], i - (RING - 1))
                sp.dma_start(m["tab"][:, u, :, :], slots).then_inc(m["deg_tab"][u], 16)
            rounds(sp, body, 0, NGD // RING, RING)
            sp.wait_ge(m["g_ready"], 1)
            sp.dma_start(node_tiles(m["g_dram"]), m["acc"][:, :, :]).then_inc(m["g_stored"], 16)
            sp.wait_ge(m["g_stored"], 16)

        @block.scalar
        def _(act):
            with act.Fori(0, STILES) as b:
                nc.scalar.activation(m["square"][:, :], m["tile_of"][:, :], ACT.Square, bias=m["minus_t"][:, bass.ds(b, 1)]).then_inc(m["squared"], 1)
                act.wait_ge(m["squared"], b + 1)
                nc.scalar.activation(m["mask"][:, 0, :], m["square"][:, :], ACT.Relu, bias=m["ones"][:, 0:1], scale=-1.0,
                                     accum_out=m["cnt_s"][:, bass.ds(b, 1)]).then_inc(m["counted_s"], 1)
                act.wait_ge(m["counted_s"], b + 1)
            act.wait_ge(m["deg_ready"], 1)
            nc.scalar.activation(m["std"][:, :], m["deg"][:, :], ACT.Sqrt).then_inc(m["deg_root"], 1)

        @block.vector
        def _(dve):
            c = Chain(dve, m["dve_chain"], m["chain_at"])

            def body(i, u, r):
                dve.wait_ge(m["deg_tab"][u], r * 16 + 16)
                need(dve, m["deg_summed"], i - (RING - 1))
                one_hot(dve, m["hot_b"][:, u, :, :], row_of(m["iota_n"][:, :], [P, 1, P]), m["tab"][:, u, :, 1:2],
                        m["node_d"][:, bass.ds(i, 1)], [P, GC, P]).then_inc(m["deg_hot"], 1)
            rounds(dve, body, 0, NGD // RING, RING)
            dve.wait_ge(m["deg_summed"], NGD)
            c(dve.tensor_copy(m["at_f"][:, :], m["bank"][7][:, 0:NGD]))
            c(dve.memset(m["deg"][:, :], 0.0))
            with dve.Fori(0, TILES) as b:
                dve.scalar_tensor_tensor(out=m["past"][:, 0:NGD], in0=m["tile_d"][:, :], scalar=m["iota_t"][:, bass.ds(b, 1)], in1=m["at_f"][:, :],
                                         op0=ALU.is_equal, op1=ALU.mult, accum_out=m["deg"][:, bass.ds(b, 1)]).then_inc(m["deg_added"], 1)
                dve.wait_ge(m["deg_added"], b + 1)
            dve.tensor_scalar(m["deg"][:, :], m["deg"][:, :], 1.0, None, ALU.add).then_inc(m["deg_ready"], 1)
            dve.wait_ge(m["deg_root"], 1)
            c(dve.reciprocal(m["dinv"][:, :], m["std"][:, :]))
            dve.tensor_tensor(m["acc"][:, :, :], m["acc"][:, :, :], column(m["dinv"][:, :], [P, NT, D]), ALU.mult).then_inc(m["g_ready"], 1)
            m["chain_at"] = c.n

        @block.tensor
        def _(pe):
            def body(i, u, r):
                pe.wait_ge(m["deg_hot"], i + 1)
                for j in range(GC):
                    last = pe.matmul(m["bank"][7][:, bass.ds(i, 1)], m["hot_b"][:, u, j, :], m["ones_b"][:, 0:1], start=(j == 0), stop=(j == GC - 1))
                last.then_inc(m["deg_summed"], 1)
            rounds(pe, body, 0, NGD // RING, RING)
            count_sums(nc, m, pe, m["cnt_s"], STILES, m["counted_s"], STILES, m["sums_s"])


def gather(m, pool, rows, source, u, gathered):
    for j in range(GC):
        pool.indirect_dma_start(out=rows[:, u, j, :], out_offset=None, in_=source,
                                in_offset=bass.IndirectOffsetOnAxis(ap=m["tab"][:, u, j, 0:1], axis=0)).then_inc(gathered[u], 16)


def layer0_block(nc, m):
    placing = STILES // PLACED_PER_ROUND
    every = RING // PLACED_PER_ROUND

    def all_rounds(eng, group, place):
        def both(i, u, r):
            group(i, u, r)
            if u % every == every - 1:
                k = u // every
                place(r * PLACED_PER_ROUND + k, k, r)
        rounds(eng, both, 0, placing, RING)
        rounds(eng, group, placing, NGD // RING, RING)

    with nc.Block() as block:
        @block.sync
        def _(sp):
            def body(i, u, r):
                slots = layer0_slots(m, sp, i)
                apart(m, sp, m["l0_hot"], i - (RING - 1))
                apart(m, sp, m["l0_gathered"][u], r * (16 * GC))
                sp.dma_start(m["tab"][:, u, :, :], slots).then_inc(m["l0_tab"][u], 16)
            rounds(sp, body, 0, NGD // RING, RING)

        @block.gpsimd
        def _(pool):
            pool.iota(m["row"][:, :].bitcast(F32), [[1, COLS]], base=NGS * SGE + 1, channel_multiplier=0,
                      allow_small_or_imprecise_dtypes=True)
            pool.iota(m["pairs"][:, :, 0:1].rearrange("p j a -> p (j a)"), [[1, COLS]], base=0, channel_multiplier=COLS).then_inc(m["junk_s"], 1)

            def body(i, u, r):
                need(pool, m["l0_summed"], i - (RING - 1))
                apart(m, pool, m["l0_tab"][u], r * 16 + 16)
                gather(m, pool, m["g_rows"], m["g_dram"], u, m["l0_gathered"])
            rounds(pool, body, 0, NGD // RING, RING)

        @block.scalar
        def _(act):
            def masks(b, k, r):
                need(act, m["mask_ready"], b)
                need(act, m["masked"], b - (PLACED_PER_ROUND - 1))
                nc.scalar.activation(m["square"][:, :], m["tile_of"][:, :], ACT.Square, bias=m["minus_t"][:, bass.ds(b, 1)]).then_inc(m["squared_p"], 1)
                act.wait_ge(m["squared_p"], b + 1)
                nc.scalar.activation(m["mask"][:, k, :], m["square"][:, :], ACT.Relu, bias=m["ones"][:, 0:1], scale=-1.0).then_inc(m["mask_ready"], 1)
            rounds(act, masks, 0, placing, PLACED_PER_ROUND)

        @block.tensor
        def _(pe):
            def group(i, u, r):
                pe.wait_ge(m["l0_hot"], i + 1)
                pe.wait_ge(m["l0_gathered"][u], r * (16 * GC) + 16 * GC)
                need(pe, m["l0_added"], i - (RING - 1))
                for j in range(GC):
                    last = pe.matmul(m["bank"][u][:, 0:D], m["hot"][:, u, j, :], m["g_rows"][:, u, j, :], start=(j == 0), stop=(j == GC - 1))
                last.then_inc(m["l0_summed"], 1)

            def place(b, k, r):
                pe.wait_ge(m["masked"], b + 1)
                for j in range(BANKS):
                    last = pe.matmul(m["bank"][4 + j][:, 0:BANK_COLS], m["ident"][:, :], m["cum"][:, k, j * BANK_COLS:(j + 1) * BANK_COLS],
                                     start=zero(b), stop=True, skip_group_check=True)
                last.then_inc(m["placed"], 1)
            pe.wait_ge(m["base_ready"], 1)
            all_rounds(pe, group, place)

        @block.vector
        def _(dve):
            c = Chain(dve, m["dve_chain"], m["chain_at"])
            n = STILES
            dve.wait_ge(m["sums_s"], 1)
            tile_groups(m, dve, c, n, SGC, m["past"][:, 0:n], m["ngi"][:, 0:n], m["first_s"][:, :], m["end_s"][:, :])
            c(dve.tensor_copy(m["used_i"][:, :], m["end_s"][:, n - 1:n]))
            c(dve.tensor_scalar(m["base_s"][:, :], m["first_s"][:, :], float(SGE), None, ALU.mult))
            dve.tensor_tensor(m["base_s"][:, :], m["base_s"][:, :], m["bank"][0][:, 0:n], ALU.add).then_inc(m["base_ready"], 1)
            dve.wait_ge(m["base_ready"], 1)

            def add(i, u):
                t = dve.value_load(m["tile_di"][0:1, bass.ds(i, 1)], min_val=0, max_val=TILES - 1)
                dve.wait_ge(m["l0_summed"], i + 1)
                need(dve, m["l0_added"], i)
                dve.tensor_tensor(m["acc"][:, bass.ds(t, 1), :], m["acc"][:, bass.ds(t, 1), :],
                                  row_of(m["bank"][u][:, 0:D], [P, 1, D]), ALU.add).then_inc(m["l0_added"], 1)

            def group(i, u, r):
                dve.wait_ge(m["l0_tab"][u], r * 16 + 16)
                need(dve, m["l0_summed"], i - (RING - 1))
                one_hot(dve, m["hot"][:, u, :, :], row_of(m["iota_n"][:, :], [P, 1, P]), m["tab"][:, u, :, 1:2],
                        m["node_d"][:, bass.ds(i, 1)], [P, GC, P]).then_inc(m["l0_hot"], 1)
                if not zero(i):
                    add(i - 1, (u - 1) % RING)

            def place(b, k, r):
                dve.wait_ge(m["mask_ready"], b + 1)
                need(dve, m["placed"], b - (PLACED_PER_ROUND - 1))
                dve.tensor_tensor_scan(m["cum"][:, k, :], m["mask"][:, k, :], m["mask"][:, k, :], m["base_s"][:, bass.ds(b, 1)],
                                       ALU.add, ALU.max).then_inc(m["scanned"], 1)
                dve.wait_ge(m["scanned"], b + 1)
                dve.tensor_tensor(m["cum"][:, k, :], m["cum"][:, k, :], m["mask"][:, k, :], ALU.mult).then_inc(m["masked"], 1)
            all_rounds(dve, group, place)
            add(NGD - 1, RING - 1)
            dve.wait_ge(m["l0_added"], NGD)
            dve.wait_ge(m["placed"], STILES)
            dve.wait_ge(m["junk_s"], 1)
            c(dve.tensor_copy(m["pairs"][:, :, 1:2], m["raw"]["src"][:, :].rearrange("p (j a) -> p j a", a=1)))
            c(dve.scalar_tensor_tensor(out=m["cum"][:, 0, :], in0=m["tile_of"][:, :], scalar=float(STILES), in1=m["row"][:, :].bitcast(F32),
                                       op0=ALU.is_ge, op1=ALU.mult))
            for j in range(BANKS):
                at = slice(j * BANK_COLS, (j + 1) * BANK_COLS)
                c(dve.tensor_tensor(m["cum"][:, 0, at], m["cum"][:, 0, at], m["bank"][4 + j][:, 0:BANK_COLS], ALU.add))
            c(dve.tensor_scalar(m["row"][:, :], m["cum"][:, 0, :], -1.0, None, ALU.add))
            m["chain_at"] = c.n



def nodes_block(nc, m):
    with nc.Block() as block:
        @block.gpsimd
        def _(pool):
            scatter(nc, m, pool, m["table_s"], m["staged_s"], m["scattered_s"])

        @block.sync
        def _(sp):
            stage(nc, m, sp, m["staged_s"], m["scattered_s"])

        @block.vector
        def _(dve):
            c = Chain(dve, m["dve_chain"], m["chain_at"])
            shape = [P, NT, D]

            def row(n):
                return row_of(m["w"][n][:, :], shape)
            c(dve.tensor_tensor(m["acc"][:, :, :], m["acc"][:, :, :], column(m["dinv"][:, :], shape), ALU.mult))
            c(dve.tensor_tensor(m["acc"][:, :, :], m["acc"][:, :, :], row("b_gcn"), ALU.add))
            normalise(nc, m, dve, c, m["acc"], m["work"], m["acc"], 2)
            c(dve.tensor_tensor(m["work"][:, :, :], m["work"][:, :, :], column(m["rstd"][:, :], shape), ALU.mult))
            c(dve.tensor_tensor(m["work"][:, :, :], m["work"][:, :, :], row("gamma"), ALU.mult))
            c(dve.tensor_tensor(m["work"][:, :, :], m["work"][:, :, :], row("beta"), ALU.add))
            c(dve.scalar_tensor_tensor(out=m["xres"][:, :, :], in0=m["work"][:, :, :], scalar=0.0, in1=m["xres"][:, :, :], op0=ALU.max, op1=ALU.add))
            normalise(nc, m, dve, c, m["xres"], m["work"], m["acc"], 3)

            def normal(i, u, r):
                need(dve, m["h2_transposed"], i - 1)
                dve.tensor_scalar(m["hs"][:, u, :], m["work"][:, bass.ds(i, 1), :], m["rstd"][:, bass.ds(i, 1)], 0.0, ALU.mult,
                                  ALU.max).then_inc(m["h2_ready"], 1)
            rounds(dve, normal, 0, NT // 2, 2)
            c(dve.memset(m["mx"][:, :], FLOOR))
            c(dve.tensor_tensor(m["xres"][:, :, :], m["xres"][:, :, :], row("bo"), ALU.add))
            c(dve.memset(m["tile_s"][:, :], 0.0))
            with dve.Fori(0, STILES - 1) as b:
                dve.scalar_tensor_tensor(out=m["tile_s"][:, :], in0=m["iota_s"][:, :], scalar=m["end_s"][:, bass.ds(b, 1)], in1=m["tile_s"][:, :],
                                         op0=ALU.is_ge, op1=ALU.add).then_inc(m["stepped_s"], 1)
                dve.wait_ge(m["stepped_s"], b + 1)
            c(dve.tensor_copy(m["tile_si"][:, :], m["tile_s"][:, :]))
            c(dve.tensor_scalar(m["node_s"][:, :], m["tile_s"][:, :], float(SN), None, ALU.mult))
            m["chain_at"] = c.n

        @block.scalar
        def _(act):
            square_root(nc, m, act, 2)
            square_root(nc, m, act, 3)

            def copies(i, u, r):
                act.wait_ge(m["h2_transposed"], i + 1)
                need(act, m["q_summed"], i - 1)
                nc.scalar.copy(m["hT"][:, u, :], m["bank"][u][:, 0:P]).then_inc(m["h2T_ready"], 1)
                act.wait_ge(m["q_summed"], i + 1)
                need(act, m["G_summed"], i - 1)
                for h in range(HEADS):
                    last = nc.scalar.activation(m["qm"][:, u, :, h, :], m["bank"][2 + u][:, 0:P].rearrange("d (q n) -> d q n", q=PARTS),
                                                ACT.Identity, bias=m["qbias"][:, h:h + 1], scale=m["qscale"][:, h:h + 1])
                last.then_inc(m["q_ready"], 1)
                act.wait_ge(m["G_summed"], i + 1)
                need(act, m["G_stored"][u], r * 16)
                nc.scalar.copy(m["gst"][:, u, :, 0:P], m["bank"][4 + u][:, :].rearrange("d (q n) -> d q n", q=PARTS)).then_inc(m["G_copied"], 1)
                nc.scalar.copy(m["gst"][:, u, :, P:P + 1], m["bank"][6 + u][:, 0:PARTS].rearrange("d (q n) -> d q n", n=1)).then_inc(m["G_ready"], 1)
                apart(m, act, m["G_copied"], i + 1)
                apart(m, act, m["G_ready"], i + 1)
                act.dma_start(m["G_dram"][bass.ds(i * (PARTS * P), PARTS * P), :].rearrange("(q d) n -> d q n", q=PARTS),
                              m["gst"][:, u, :, :]).then_inc(m["G_stored"][u], 16)
            rounds(act, copies, 0, NT // 2, 2)
            for u in range(2):
                act.wait_ge(m["G_stored"][u], NT // 2 * 16)

        @block.tensor
        def _(pe):
            def body(i, u, r):
                pe.wait_ge(m["h2_ready"], i + 1)
                need(pe, m["h2T_ready"], i - 1)
                pe.transpose(m["bank"][u][:, 0:P], m["hs"][:, u, :], m["ident"][:, :]).then_inc(m["h2_transposed"], 1)
                pe.wait_ge(m["h2T_ready"], i + 1)
                need(pe, m["q_ready"], i - 1)
                pe.matmul(m["bank"][2 + u][:, 0:P], m["w"]["Wq"][:, :], m["hT"][:, u, :], start=True, stop=True).then_inc(m["q_summed"], 1)
                pe.wait_ge(m["q_ready"], i + 1)
                need(pe, m["G_ready"], i - 1)
                q = m["qm"][:, u, :, :, :].rearrange("d q h n -> d (q h n)")
                pe.matmul(m["bank"][4 + u][:, :], m["wkT"][:, :], q, start=True, stop=True)
                for j in range(PARTS):
                    last = pe.matmul(m["bank"][6 + u][:, j:j + 1], q[:, j * P:(j + 1) * P], m["w"]["bk"][:, 0:1], start=True, stop=True)
                last.then_inc(m["G_summed"], 1)
            rounds(pe, body, 0, NT // 2, 2)



def layer1_block(nc, m):
    trK, scores, trE, sums = m["bank"][0:2], m["bank"][2:4], m["bank"][4:6], m["bank"][6:8]
    usual, all_of_them = USUAL // SRING, NGS // SRING

    def group_tile(eng, i):
        return eng.value_load(m["tile_si"][0:1, bass.ds(i, 1)], min_val=0, max_val=STILES - 1)

    def twice(eng, part):
        part(0, usual)
        with eng.If(eng.value_load(m["used_i"][0:1, 0:1], min_val=0, max_val=NGS) > USUAL):
            part(usual, all_of_them)

    def before(i, lag, first):
        return isinstance(i, int) and i < first * SRING + lag

    def ring(u):
        return u % SRING

    with nc.Block() as block:
        @block.sync
        def _(sp):
            def body(i, u, r):
                apart(m, sp, m["l1_hot"], i - (SRING - 1))
                apart(m, sp, m["l1_gathered"][u], r * (16 * SGC))
                sp.dma_start(m["tab_s"][:, u, :, :], in_partitions(m["table_s"][bass.ds(i * SGE, SGE), :])).then_inc(m["l1_tab"][u], 16)
                t = group_tile(sp, i)
                apart(m, sp, m["max_ready"], i - (SRING - 1))
                sp.dma_start(m["G"][:, u, :], m["G_dram"][bass.ds(t * P, P), :]).then_inc(m["G_loaded"][u], 16)
            twice(sp, lambda first, last: steps(sp, body, first, last, SRING))

        @block.gpsimd
        def _(pool):
            pool.memset(m["agg"][:, :, :], 0.0)
            pool.memset(m["kv_rows"][:, :, :, 2 * D:], 1.0).then_inc(m["rows_ready"], 1)

            def body(i, u, r):
                need(pool, m["l1_summed"], i - (SRING - 1))
                apart(m, pool, m["l1_tab"][u], r * 16 + 16)
                for j in range(SGC):
                    pool.indirect_dma_start(out=m["kv_rows"][:, u, j, 0:2 * D], out_offset=None, in_=m["kv"],
                                            in_offset=bass.IndirectOffsetOnAxis(ap=m["tab_s"][:, u, j, 0:1], axis=0)).then_inc(m["l1_gathered"][u], 16)
            twice(pool, lambda first, last: steps(pool, body, first, last, SRING))

        @block.tensor
        def _(pe):
            def score(i, u, r):
                k = u % 2
                pe.wait_ge(m["l1_hot"], i + 1)
                need(pe, m["exp_ready"], i - 1)
                for j in range(SGC):
                    pe.matmul(scores[k][:, j * P:(j + 1) * P], m["others"][:, u, j, :], m["out_b"][:, :], start=(j == 0), stop=False, skip_group_check=True)
                pe.wait_ge(m["kT_ready"], i + 1)
                pe.wait_ge(m["G_loaded"][u], r * 16 + 16)
                pe.matmul(scores[k][:, 0:SGE], m["G"][:, u, 0:P], m["kT"][:, k, :], start=False, stop=True, skip_group_check=True).then_inc(m["scored"], 1)

            def keys(i, u, r):
                pe.wait_ge(m["l1_gathered"][u], r * (16 * SGC) + 16 * SGC)
                need(pe, m["kT_ready"], i - 1)
                for j in range(SGC):
                    last = pe.transpose(trK[u % 2][:, j * P:(j + 1) * P], m["kv_rows"][:, u, j, 0:D], m["ident"][:, :])
                last.then_inc(m["k_transposed"], 1)

            def weights(i, u):
                pe.wait_ge(m["exp_ready"], i + 1)
                need(pe, m["eT_ready"], i - 1)
                for j in range(SGC):
                    last = pe.transpose(trE[u % 2][:, j * P:(j + 1) * P], m["ex"][:, u % 2, j * P:(j + 1) * P], m["ident"][:, :])
                last.then_inc(m["e_transposed"], 1)

            def add_up(i, u):
                pe.wait_ge(m["eT_ready"], i + 1)
                need(pe, m["l1_added"], i - 1)
                for j in range(SGC):
                    last = pe.matmul(sums[u % 2][:, 0:VW], m["exT"][:, u % 2, j * P:(j + 1) * P], m["kv_rows"][:, u, j, D:D + VW],
                                     start=(j == 0), stop=(j == SGC - 1))
                last.then_inc(m["l1_summed"], 1)

            def part(first, last):
                end = last * SRING

                def body(i, u, r):
                    score(i, u, r)
                    if not (isinstance(i, int) and i == end - 1):
                        keys(i + 1, ring(u + 1), r if u < SRING - 1 else r + 1)
                    if not before(i, 1, first):
                        weights(i - 1, ring(u - 1))
                    if not before(i, 2, first):
                        add_up(i - 2, ring(u - 2))
                keys(first * SRING, 0, first)
                steps(pe, body, first, last, SRING)
                weights(end - 1, SRING - 1)
                add_up(end - 2, SRING - 2)
                add_up(end - 1, SRING - 1)
            pe.wait_ge(m["rows_ready"], 1)
            twice(pe, part)

        @block.scalar
        def _(act):
            def keys(i, u):
                act.wait_ge(m["k_transposed"], i + 1)
                need(act, m["scored"], i - 1)
                nc.scalar.copy(m["kT"][:, u % 2, :], trK[u % 2][:, 0:SGE]).then_inc(m["kT_ready"], 1)

            def weights(i, u):
                act.wait_ge(m["e_transposed"], i + 1)
                need(act, m["l1_summed"], i - 1)
                nc.scalar.copy(m["exT"][:, u % 2, :], trE[u % 2][:, 0:SGE]).then_inc(m["eT_ready"], 1)

            def exponentials(i, u):
                act.wait_ge(m["max_ready"], i + 1)
                need(act, m["l1_added"], i - (SRING - 1))
                nc.scalar.activation(m["decay"][:, u:u + 1], m["drop"][:, u:u + 1], ACT.Exp).then_inc(m["decay_ready"], 1)
                need(act, m["e_transposed"], i - 1)
                nc.scalar.activation(m["ex"][:, u % 2, :], scores[u % 2][:, 0:SGE], ACT.Exp, bias=m["shift"][:, u:u + 1]).then_inc(m["exp_ready"], 1)

            def part(first, last):
                end = last * SRING

                def body(i, u, r):
                    if not (isinstance(i, int) and i == end - 1):
                        keys(i + 1, ring(u + 1))
                    if not before(i, 1, first):
                        weights(i - 1, ring(u - 1))
                    exponentials(i, u)
                keys(first * SRING, 0)
                steps(act, body, first, last, SRING)
                weights(end - 1, SRING - 1)
            twice(act, part)

        @block.vector
        def _(dve):
            tiles = {}

            def hot(i, u, r):
                dve.wait_ge(m["l1_tab"][u], r * 16 + 16)
                need(dve, m["scored"], i - (SRING - 1))
                one_hot(dve, m["others"][:, u, :, :], row_of(m["iota_h"][:, :], [P, 1, P]), m["tab_s"][:, u, :, 1:2],
                        m["node_s"][:, bass.ds(i, 1)], [P, SGC, P], ALU.not_equal).then_inc(m["l1_hot"], 1)

            def maxima(i, u, r):
                t = group_tile(dve, i)
                tiles[u] = t
                at = slice(u, u + 1)
                need(dve, m["exp_ready"], i - (SRING - 1))
                apart(m, dve, m["scored"], i + 1)
                dve.tensor_reduce(m["gmax"][:, at], scores[u % 2][:, 0:SGE], AX_X, ALU.max).then_inc(m["reduced"], 1)
                c, mx = m["G"][:, u, P:P + 1], m["mx"][:, bass.ds(t, 1)]
                dve.wait_ge(m["G_loaded"][u], r * 16 + 16)
                need(dve, m["max_ready"], i)
                dve.wait_ge(m["reduced"], i + 1)
                dve.scalar_tensor_tensor(out=m["mnew"][:, at], in0=m["gmax"][:, at], scalar=c, in1=mx, op0=ALU.add,
                                         op1=ALU.max).then_inc(m["maxing"], 1)
                dve.wait_ge(m["maxing"], i + 1)
                dve.tensor_tensor(m["drop"][:, at], mx, m["mnew"][:, at], ALU.subtract).then_inc(m["dropped"], 1)
                dve.tensor_tensor(m["shift"][:, at], c, m["mnew"][:, at], ALU.subtract).then_inc(m["shifted"], 1)
                dve.wait_ge(m["dropped"], i + 1)
                dve.scalar_tensor_tensor(out=mx, in0=m["gmax"][:, at], scalar=c, in1=mx, op0=ALU.add,
                                         op1=ALU.max).then_inc(m["max_ready"], 1)

            def add(i, u, t):
                dve.wait_ge(m["decay_ready"], i + 1)
                need(dve, m["l1_added"], i)
                dve.wait_ge(m["l1_summed"], i + 1)
                agg = m["agg"][:, bass.ds(t, 1), :]
                dve.scalar_tensor_tensor(out=agg, in0=agg, scalar=m["decay"][:, u:u + 1], in1=row_of(sums[u % 2][:, 0:VW], [P, 1, VW]),
                                         op0=ALU.mult, op1=ALU.add).then_inc(m["l1_added"], 1)

            def part(first, last):
                end = last * SRING

                def body(i, u, r):
                    maxima(i, u, r)
                    if not (isinstance(i, int) and i >= end - 2):
                        hot(i + 2, ring(u + 2), r if u < SRING - 2 else r + 1)
                    if not before(i, 2, first):
                        add(i - 2, ring(u - 2), tiles[u - 2] if u >= 2 else group_tile(dve, i - 2))
                hot(first * SRING, 0, first)
                hot(first * SRING + 1, 1, first)
                steps(dve, body, first, last, SRING)
                add(end - 2, SRING - 2, tiles[SRING - 2])
                add(end - 1, SRING - 1, tiles[SRING - 1])
                dve.wait_ge(m["l1_added"], end)
            dve.wait_ge(m["rows_ready"], 1)
            twice(dve, part)


def output_block(nc, m):
    trA, outs, trH = m["bank"][0:2], m["bank"][2:4], m["bank"][4:6]

    def tiles_of_nodes(eng, body):
        body(0, 0)
        with eng.Fori(0, TILES // 2) as r:
            body(r * 2 + 1, 1)
            body(r * 2 + 2, 0)

    with nc.Block() as block:
        @block.vector
        def _(dve):
            c = Chain(dve, m["dve_chain"], m["chain_at"])
            c(dve.tensor_scalar(m["rl"][:, :], m["agg"][:, :, D:VW].rearrange("p t a -> p (t a)"), 0.5, None, ALU.max))
            c(dve.reciprocal(m["rl"][:, :], m["rl"][:, :]))

            def own(i, u):
                need(dve, m["a_transposed"], i - 1)
                dve.tensor_tensor(m["y"][:, u, :, :], m["agg"][:, bass.ds(i * PARTS, PARTS), :],
                                  column(m["rl"][:, bass.ds(i * PARTS, PARTS)], [P, PARTS, VW]), ALU.mult).then_inc(m["y_ready"], 1)
                if not zero(i):
                    add(i - 1, 1 - u)

            def add(i, u):
                dve.wait_ge(m["o_summed"], i + 1)
                xr = m["xres"][:, bass.ds(i, 1), :]
                dve.tensor_tensor(xr, xr, row_of(outs[u][:, 0:D], [P, 1, D]), ALU.add).then_inc(m["o_added"], 1)
            tiles_of_nodes(dve, own)
            add(TILES - 1, 0)

        @block.scalar
        def _(act):
            def copies(i, u):
                act.wait_ge(m["a_transposed"], i + 1)
                need(act, m["o_summed"], i - 1)
                for h in range(HEADS):
                    nc.scalar.copy(m["aT"][:, u, h, :].rearrange("d (q n) -> d q n", q=PARTS),
                                   trA[u][:, :].rearrange("d (q g n) -> d q g n", q=PARTS, g=HEADS)[:, :, h, :])
                nc.scalar.copy(m["has"][:, u, :], trH[u][0:1, 0:P]).then_inc(m["aT_ready"], 1)
            tiles_of_nodes(act, copies)

        @block.tensor
        def _(pe):
            def body(i, u):
                pe.wait_ge(m["y_ready"], i + 1)
                need(pe, m["aT_ready"], i - 1)
                for q in range(PARTS):
                    pe.transpose(trA[u][:, q * P:(q + 1) * P], m["y"][:, u, q, 0:D], m["ident"][:, :])
                    last = pe.matmul(trH[u][0:1, q * SN:(q + 1) * SN], m["y"][:, u, q, D:VW], m["ident"][:, 0:SN], start=True, stop=True)
                last.then_inc(m["a_transposed"], 1)
                pe.wait_ge(m["aT_ready"], i + 1)
                need(pe, m["o_added"], i - 1)
                for h in range(HEADS):
                    pe.matmul(outs[u][:, 0:D], m["aT"][:, u, h, :], m["wvo"][:, h * D:(h + 1) * D], start=(h == 0), stop=False)
                pe.matmul(outs[u][:, 0:D], m["has"][:, u, :], m["bvo"][:, :], start=False, stop=True).then_inc(m["o_summed"], 1)
            tiles_of_nodes(pe, body)

        @block.sync
        def _(sp):
            sp.wait_ge(m["o_added"], TILES)
            sp.dma_start(node_tiles(m["out"][0:N // P * P, :]), m["xres"][:, 0:N // P, :]).then_inc(m["out_stored"], 16)
            sp.dma_start(m["out"][N // P * P:N, :], m["xres"][0:N % P, N // P, :]).then_inc(m["out_stored"], 16)
            sp.wait_ge(m["out_stored"], 32)


SEMAPHORES = """
    held paddings consts keys_loaded x_loaded w_loaded emptied emptied_d pool_chain dve_chain unsorted_chain
    sqrt_asked sqrt_done pairs_ready pairs_stored counted_d sums_d stepped w_transposed wT_ready w12_summed w12_ready
    h_ready h_transposed hT_ready hw_summed hw_read junk_d placed_d rows_d
    deg_hot deg_summed deg_added deg_ready deg_root g_ready g_stored squared counted_s sums_s
    l0_hot l0_summed l0_added junk_s squared_p mask_ready scanned masked placed base_ready
    h2_ready h2_transposed h2T_ready q_summed q_ready G_summed G_copied G_ready stepped_s
    wo_masked wvo_summed wvo_ready rows_ready l1_hot k_transposed kT_ready scored reduced maxing dropped shifted max_ready
    decay_ready exp_ready e_transposed eT_ready l1_summed l1_added y_ready a_transposed aT_ready o_summed o_added out_stored
""".split()
SEMAPHORE_RINGS = {"deg_tab": RING, "l0_tab": RING, "l0_gathered": RING, "l1_tab": SRING, "l1_gathered": SRING,
                   "G_stored": 2, "G_loaded": SRING, "staged_d": 2, "staged_s": 2, "scattered_d": 2, "scattered_s": 2}
EMPTY = COLS // 2


def gnn_kernel(nc, x, src, dst, kv, W_lin, W_gcn, b_gcn, gamma, beta, Wq, bq, Wk, bk, Wv, bv, Wo, bo, out):
    m = dict(x=x, kv=kv, out=out, keys={"dst": dst, "src": src})
    m["arg"] = {"W_lin": W_lin, "W_gcn": W_gcn, "Wq": Wq, "Wk": Wk, "Wv": Wv, "Wo": Wo, "bq": bq, "bk": bk,
             "b_gcn": b_gcn, "gamma": gamma, "beta": beta, "bv": bv, "bo": bo}
    m["table_d"] = nc.dram_tensor("table_d", (SORTED_AT + NGD * GE + COLS, 2), I32).ap()
    m["table_s"] = nc.dram_tensor("table_s", (NGS * SGE + COLS, 2), I32).ap()
    m["g_dram"] = nc.dram_tensor("g_dram", (NT * P, D), F32).ap()
    m["G_dram"] = nc.dram_tensor("G_dram", (NT * PARTS * P, P + 1), F32).ap()

    with ExitStack() as whole:
        def place(stack, name, shape, dt=F32):
            return stack.enter_context(nc.sbuf_tensor(name, shape, dt))

        for name in SEMAPHORES:
            m[name] = whole.enter_context(nc.semaphore(name))
        for name, n in SEMAPHORE_RINGS.items():
            m[name] = [whole.enter_context(nc.semaphore(f"{name}{i}")) for i in range(n)]
        m["bank"] = [whole.enter_context(nc.psum_tensor(f"bank{i}", [P, 512], F32)) for i in range(8)]

        for name, shape, dt in (
                ("ident", [P, P], F32), ("ones", [P, P], F32), ("iota_n", [P, P], F32), ("iota_h", [P, P], F32), ("headmask", [P, HEADS], F32),
                ("out_b", [P, P], BF16), ("wvo", [P, HEADS * D], F32), ("bvo", [1, D], F32), ("used_i", [P, 1], I32),
                ("wkT", [P, D], F32), ("xres", [P, NT, D], F32), ("mx", [P, STILES], F32), ("hT", [P, 2, P], F32),
                ("tab", [P, RING, GC, 2], I32), ("tab_s", [P, SRING, SGC, 2], I32),
                ("tile_si", [P, NGS], I32), ("node_s", [P, NGS], F32)):
            m[name] = place(whole, name, shape, dt)
        m["w"] = {n: place(whole, f"w_{n}", [P, D if n not in ("bq", "bk", "bv") else 1]) for n in m["arg"]}

        with ExitStack() as front:
            small = ("stat", "mean", "var", "std", "rstd", "deg", "dinv")
            for name, shape, dt in (
                    *((n, [P, NT], F32) for n in small), ("flags", [P, 4], F32), ("flags_i", [P, 1], I32),
                    ("qscale", [P, HEADS], F32), ("qbias", [P, HEADS], F32), ("ones_b", [P, 2], BF16),
                    ("before", [P, P], F32), ("wvT", [P, D], F32), ("wo_heads", [P, HEADS, D], F32), ("w_linT", [P, D], F32), ("w12", [P, D], F32), ("hs", [P, 2, D], F32),
                    ("iota_d", [P, NGD], F32), ("iota_s", [P, NGS], F32), ("iota_t", [P, STILES], F32), ("minus_t", [P, STILES], F32),
                    ("cnt", [P, 64], F32), ("ng", [P, 64], F32), ("first_d", [P, 64], F32), ("base_d", [P, 64], F32),
                    ("end", [P, 64], F32), ("adj", [P, 64], F32), ("step", [P, 64], F32), ("tot", [P, 64], F32),
                    ("ngi", [P, STILES], I32), ("cnt_s", [P, STILES], F32), ("first_s", [P, STILES], F32),
                    ("end_s", [P, STILES], F32), ("base_s", [P, STILES], F32), ("past", [P, NGS], F32),
                    ("at_f", [P, NGD], F32), ("at_d", [P, NGD], I32), ("tile_d", [P, NGD], F32), ("tile_di", [P, NGD], I32),
                    ("node_d", [P, NGD], F32), ("tile_s", [P, NGS], F32),
                    ("row_st", [P, 2, SC], I32), ("pair_st", [P, 2, SC, 2], I32),
                    ("work", [P, NT, D], F32), ("acc", [P, NT, D], F32),
                    ("tile_of", [P, COLS], F32), ("row", [P, COLS], I32), ("pairs", [P, COLS, 2], I32)):
                m[name] = place(front, name, shape, dt)
            with ExitStack() as sorting:
                for name, shape, dt in (
                        ("square", [P, COLS], F32), ("mask", [P, 2, COLS], F32), ("cum", [P, 2, COLS], F32),
                        ("g_rows", [P, RING, GC, D], F32)):
                    m[name] = place(sorting, name, shape, dt)
                m["raw"] = {k: place(sorting, f"raw_{k}", [P, COLS], I32) for k in ("dst", "src")}
                m["next"] = m["cum"][:, 1, :].bitcast(I32)
                m["empty"] = m["g_rows"][:, :, :, :].rearrange("p u c d -> p (u c d)")[:, 0:2 * EMPTY].bitcast(I32).rearrange("p (j w) -> p j w", w=2)
                m["hot"] = m["work"][:, 0:RING * GC, :].rearrange("p (u c) n -> p u c n", u=RING)
                m["hot_b"] = m["work"][:, 0:RING * GC // 2, :].rearrange("p t n -> p (t n)").bitcast(BF16).rearrange("p (u c n) -> p u c n", u=RING, c=GC)
                first_block(nc, m)
                unsorted_block(nc, m)
                degree_block(nc, m)
                layer0_block(nc, m)
            for name, shape, dt in (("qm", [P, 2, PARTS, HEADS, SN], F32), ("gst", [P, 2, PARTS, P + 1], F32)):
                m[name] = place(front, name, shape, dt)
            nodes_block(nc, m)
        with ExitStack() as back:
            for name, shape, dt in (
                    ("agg", [P, STILES, VW], F32), ("kv_rows", [P, SRING, SGC, D + VW], F32), ("G", [P, SRING, P + 1], F32),
                    ("others", [P, SRING, SGC, P], BF16), ("kT", [P, 2, SGE], F32), ("ex", [P, 2, SGE], F32), ("exT", [P, 2, SGE], F32),
                    ("aT", [P, 2, HEADS, P], F32), ("has", [1, 2, P], F32), ("y", [P, 2, PARTS, VW], F32), ("rl", [P, STILES], F32),
                    *((n, [P, SRING], F32) for n in ("gmax", "mnew", "drop", "shift", "decay"))):
                m[name] = place(back, name, shape, dt)
            layer1_block(nc, m)
            output_block(nc, m)


_VECTORS = {"W_lin": "L0_gnn_W_lin", "W_gcn": "L0_gnn_W_gcn", "b_gcn": "L0_gnn_b_gcn", "gamma": "L0_gnn_gamma",
            "beta": "L0_gnn_beta", "Wq": "L1_gnn_Wq", "bq": "L1_gnn_bq", "Wk": "L1_gnn_Wk", "bk": "L1_gnn_bk",
            "Wv": "L1_gnn_Wv", "bv": "L1_gnn_bv", "Wo": "L1_gnn_Wo", "bo": "L1_gnn_bo"}


def kernel(**inputs):
    import numpy as _np
    import concourse.bacc as _bacc
    from concourse import mybir as _mybir
    from concourse.bass_utils import run_bass_kernel_spmd as _run

    nc = _bacc.Bacc("TRN2", target_bir_lowering=False, num_devices=1)
    host = {"x": inputs["x"], "src": inputs["src"], "dst": inputs["dst"],
            "kv": _np.concatenate([_np.asarray(inputs["edge_attr_128"]), _np.asarray(inputs["edge_attr_128_n2"])], axis=1)}
    host.update({short: inputs[name] for short, name in _VECTORS.items()})
    arrays, args = {}, {}
    for name, value in host.items():
        a = _np.ascontiguousarray(value)
        arrays[f"in_{name}"] = a
        args[name] = nc.dram_tensor(f"in_{name}", a.shape, _mybir.dt.from_np(a.dtype), kind="ExternalInput").ap()
    args["out"] = nc.dram_tensor("out", (N, D), F32, kind="ExternalOutput").ap()
    gnn_kernel(nc, **args)
    r = _run(nc, [arrays], core_ids=[0])
    return r.results[0]["out"]
```

```python
from contextlib import ExitStack

import concourse.bass as bass
from concourse import mybir

F32 = mybir.dt.float32
I32 = mybir.dt.int32
BF16 = mybir.dt.bfloat16
ALU = mybir.AluOpType
ACT = mybir.ActivationFunctionType
AX_X = mybir.AxisListType.X

P = 128
D = 128
N = 6250
E = 206250
HEADS = 4
DH = D // HEADS
SCALE = float(DH) ** -0.5
EPS = 1e-5

TILES = -(-N // P)
NT = TILES + TILES % 2
SN = P // HEADS
PARTS = P // SN
STILES = -(-N // SN)
COLS = 1616
SC = 8
GC = 4
GE = GC * P
RING = 4
SGC = 3
SGE = SGC * P
SRING = 6
VW = D + 1


def groups(tiles, slots, ring):
    n = -(-(E + tiles * (slots - 1)) // slots)
    return n + -n % ring


NGD = groups(TILES, GE, RING)
NGS = groups(STILES, SGE, SRING)
USUAL = STILES * -(-E // (STILES * SGE))
USUAL += -USUAL % SRING
PAD_KEY = P * P - 1
BIG = 2.0 ** 100
FLOOR = -1.0e29
FULL = E // COLS
REST = E - FULL * COLS
EDGES = P * COLS
SORTED_AT = EDGES + GE
NEXT_OUT_OF_ORDER = 63
PLACED_PER_ROUND = 2
BANKS = 4
BANK_COLS = COLS // BANKS
LOADS_W = 13
HC = 16
HOT_STEPS = COLS // HC
COUNTS = STILES + 2
COUNTS_PER_TILE = COUNTS // NT
COUNTS_FIRST = (COUNTS - COUNTS_PER_TILE * NT) * 2 // 3
COUNTS_LAST = COUNTS_FIRST + COUNTS_PER_TILE * NT
assert EDGES >= E and COLS % (2 * SC) == 0 and COLS % HC == 0 and HOT_STEPS == 2 * NT + 1 and PAD_KEY // P >= TILES and COLS % BANKS == 0 and BANK_COLS <= 512
assert STILES % PLACED_PER_ROUND == 0 and STILES // PLACED_PER_ROUND <= NGD // RING and STILES == PARTS * TILES


def need(eng, sem, count):
    if not isinstance(count, int) or count > 0:
        eng.wait_ge(sem, count)


def apart(m, eng, sem, count):
    if not isinstance(count, int) or count > 0:
        eng.wait_ge(sem, count)
        eng.sem_inc(m["held"], 1)


def steps(eng, body, first, last, unroll):
    for u in range(unroll):
        body(first * unroll + u, u, first)
    with eng.Fori(first + 1, last - 1) as r:
        for u in range(unroll):
            body(r * unroll + u, u, r)
    for u in range(unroll):
        body((last - 1) * unroll + u, u, last - 1)


def rounds(eng, body, first, last, unroll):
    if first == 0:
        for u in range(unroll):
            body(u, u, 0)
    with eng.Fori(max(first, 1), last) as r:
        for u in range(unroll):
            body(r * unroll + u, u, r)


def registers(nc, engine, at):
    _, values = nc.values_load_multi_w_load_instructions(
        at[0], engines=[engine], min_val=0, max_val=at[1],
        skip_runtime_bounds_check_because="the program computes them, in range for any inputs")
    return values


def zero(i):
    return isinstance(i, int) and i == 0


class Chain:

    def __init__(self, eng, sem, start=0):
        self.eng, self.sem, self.n = eng, sem, start

    def __call__(self, ins):
        ins.then_inc(self.sem, 1)
        self.n = self.n + 1
        self.eng.wait_ge(self.sem, self.n)


def column(ap, shape):
    return ap.rearrange("p (t a) -> p t a", a=1).to_broadcast(shape)


def row_of(ap, shape):
    return ap.rearrange("p (a d) -> p a d", a=1).to_broadcast(shape)


def node_tiles(ap):
    return ap.rearrange("(t p) d -> p t d", p=P)


def in_partitions(ap):
    return ap.rearrange("(p c) w -> p c w", p=P)



def load(nc, m, sp):
    sp.wait_ge(m["paddings"], 1)
    dst, src = m["keys"]["dst"], m["keys"]["src"]
    for t, k, shift in ((m["raw"]["dst"], dst, 0), (m["next"], dst, 1), (m["raw"]["src"], src, 0)):
        sp.dma_start(t[0:FULL // 16 * 16, :], k[shift:shift + FULL // 16 * 16 * COLS].rearrange("(p j) -> p j", j=COLS)).then_inc(m["keys_loaded"], 16)
        sp.dma_start(t[FULL // 16 * 16:FULL, :], k[shift + FULL // 16 * 16 * COLS:shift + FULL * COLS].rearrange("(p j) -> p j", j=COLS)).then_inc(m["keys_loaded"], 16)
        sp.dma_start(t[FULL:FULL + 1, 0:REST - shift], k[shift + FULL * COLS:E].rearrange("(a j) -> a j", a=1)).then_inc(m["keys_loaded"], 16)
    sp.dma_start(m["xres"][:, 0:N // P, :], node_tiles(m["x"][0:N // P * P, :])).then_inc(m["x_loaded"], 16)
    sp.dma_start(m["xres"][0:N % P, N // P, :], m["x"][N // P * P:N, :]).then_inc(m["x_loaded"], 16)
    for n in ("W_lin", "W_gcn", "Wq", "Wk", "Wv", "Wo"):
        sp.dma_start(m["w"][n][:, :], m["arg"][n]).then_inc(m["w_loaded"], 16)
    for n in ("bq", "bk", "bv"):
        sp.dma_start(m["w"][n][:, :], m["arg"][n].rearrange("(p a) -> p a", a=1)).then_inc(m["w_loaded"], 16)
    for n in ("b_gcn", "gamma", "beta", "bo"):
        sp.dma_start(m["w"][n][:, :], m["arg"][n].rearrange("(a d) -> a d", a=1).to_broadcast([P, D])).then_inc(m["w_loaded"], 16)


def constants(nc, m, pool):
    c = Chain(pool, m["pool_chain"])
    for t in (m["raw"]["dst"], m["next"], m["raw"]["src"]):
        pool.memset(t[:, :], PAD_KEY)
    pool.memset(m["xres"][:, N // P:NT, :], 0.0)
    pool.memset(m["cnt"][:, :], 0.0).then_inc(m["paddings"], 1)
    pool.memset(m["ones"][:, :], 1.0)
    pool.memset(m["empty"][:, :, 0:1], 0)
    pool.memset(m["empty"][:, :, 1:2], PAD_KEY)
    for t, sign in ((m["iota_d"], 1), (m["iota_s"], 1), (m["iota_n"], 1), (m["iota_t"], 1), (m["minus_t"], -1)):
        pool.iota(t[:, :], [[sign, t.shape[1]]], base=0, channel_multiplier=0, allow_small_or_imprecise_dtypes=True)
    pool.iota(m["one_minus_t"][:, :], [[-1, COUNTS]], base=1, channel_multiplier=0, allow_small_or_imprecise_dtypes=True)
    pool.iota(m["iota_h"][:, :], [[0, HEADS], [1, SN]], base=0, channel_multiplier=0, allow_small_or_imprecise_dtypes=True)
    c(pool.memset(m["headmask"][:, :], 1.0))
    c(pool.memset(m["out_b"][:, :], 0.0))
    c(pool.memset(m["ident"][:, :], 0.0))
    c(pool.memset(m["before"][:, :], 1.0))
    pool.affine_select(out=m["ident"][:, :], in_=m["ident"][:, :], compare_op=ALU.not_equal, fill=1.0, base=0,
                       pattern=[[-1, P]], channel_multiplier=1)
    pool.affine_select(out=m["before"][:, :], in_=m["before"][:, :], compare_op=ALU.is_gt, fill=0.0, base=0,
                       pattern=[[1, P]], channel_multiplier=-1)
    c(pool.affine_select(out=m["out_b"][:, :], in_=m["out_b"][:, :], compare_op=ALU.not_equal, fill=-BIG, base=0,
                         pattern=[[-1, P]], channel_multiplier=1))
    c(pool.affine_select(out=m["headmask"][:, :], in_=m["headmask"][:, :], compare_op=ALU.is_ge, fill=0.0, base=0,
                         pattern=[[-DH, HEADS]], channel_multiplier=1))
    pool.affine_select(out=m["headmask"][:, :], in_=m["headmask"][:, :], compare_op=ALU.is_ge, fill=0.0, base=DH - 1,
                       pattern=[[DH, HEADS]], channel_multiplier=-1).then_inc(m["consts"], 1)


def normalise(nc, m, dve, c, src, centred, squares, turn):
    shape = [P, NT, D]
    c(dve.tensor_reduce(m["stat"][:, :], src[:, :, :], AX_X, ALU.add))
    c(dve.tensor_scalar(m["mean"][:, :], m["stat"][:, :], 1.0 / D, None, ALU.mult))
    c(dve.tensor_tensor(centred[:, :, :], src[:, :, :], column(m["mean"][:, :], shape), ALU.subtract))
    c(dve.tensor_tensor(squares[:, :, :], centred[:, :, :], centred[:, :, :], ALU.mult))
    c(dve.tensor_reduce(m["stat"][:, :], squares[:, :, :], AX_X, ALU.add))
    dve.tensor_scalar(m["var"][:, :], m["stat"][:, :], 1.0 / D, EPS, ALU.mult, ALU.add).then_inc(m["sqrt_asked"], 1)
    dve.wait_ge(m["sqrt_done"], turn)
    dve.reciprocal(m["rstd"][:, :], m["std"][:, :]).then_inc(m["norm_ready"], 1)
    dve.wait_ge(m["norm_ready"], turn)


def square_root(nc, m, act, turn):
    act.wait_ge(m["sqrt_asked"], turn)
    nc.scalar.activation(m["std"][:, :], m["var"][:, :], ACT.Sqrt).then_inc(m["sqrt_done"], 1)


def tile_groups(dve, c, totals, gc, ng, ngi, first, end):
    c(dve.tensor_scalar(ng, totals, float(gc * P - 1), None, ALU.add))
    c(dve.tensor_copy(ngi, ng))
    c(dve.tensor_scalar(ngi, ngi, P.bit_length() - 1, None, ALU.arith_shift_right))
    c(dve.tensor_copy(ng, ngi))
    c(dve.tensor_scalar(ng, ng, float(-(-2 ** 13 // gc)), None, ALU.mult))
    c(dve.tensor_copy(ngi, ng))
    c(dve.tensor_scalar(ngi, ngi, 13, None, ALU.arith_shift_right))
    c(dve.tensor_copy(ng, ngi))
    c(dve.memset(first, 0.0))
    c(dve.tensor_tensor_scan(end, ng, first, 0.0, ALU.add, ALU.add))
    c(dve.tensor_tensor(first, end, ng, ALU.subtract))


def first_block(nc, m):
    with nc.Block() as block:
        @block.sync
        def _(sp):
            load(nc, m, sp)
            sp.wait_ge(m["pairs_ready"], 1)
            sp.dma_start(in_partitions(m["table_d"][0:EDGES, :]), m["pairs"][:, :, :]).then_inc(m["pairs_stored"], 16)
            sp.dma_start(in_partitions(m["table_d"][EDGES:EDGES + GE, :]), m["empty"][:, 0:GE // P, :]).then_inc(m["pairs_stored"], 16)
            t3 = in_partitions(m["table_s"][0:NGS * SGE, :])
            for j in range(0, NGS * SGC, EMPTY):
                n = min(EMPTY, NGS * SGC - j)
                sp.dma_start(t3[:, j:j + n, :], m["empty"][:, 0:n, :]).then_inc(m["emptied"], 16)
            sp.wait_ge(m["g_ready"], 1)
            sp.dma_start(node_tiles(m["g_dram"]), m["acc"][:, :, :]).then_inc(m["g_stored"], 16)
            sp.wait_ge(m["g_stored"], 16)
            sp.wait_ge(m["pairs_stored"], 32)
            sp.wait_ge(m["emptied"], 16 * -(-NGS * SGC // EMPTY))

        @block.gpsimd
        def _(pool):
            constants(nc, m, pool)

        @block.vector
        def _(dve):
            c = Chain(dve, m["dve_chain"])
            dve.wait_ge(m["consts"], 1)
            dve.wait_ge(m["keys_loaded"], 16 * 9)
            c(dve.tensor_scalar(m["mask"][:, 0, :].bitcast(I32), m["raw"]["src"][:, :], SN.bit_length() - 1, None, ALU.arith_shift_right))
            dve.tensor_copy(m["tile_of"][:, :], m["mask"][:, 0, :].bitcast(I32)).then_inc(m["tile_of_ready"], 1)
            dve.wait_ge(m["tile_of_ready"], 1)
            one = "p (j a) -> p j a"
            dve.tensor_copy(m["pairs"][:, :, 1:2], m["raw"]["dst"][:, :].rearrange(one, a=1))
            dve.tensor_scalar(m["pairs"][:, :, 0:1], m["raw"]["src"][:, :].rearrange(one, a=1), float(NT * P - 1), None, ALU.min).then_inc(m["pairs_ready"], 1)
            c(dve.tensor_tensor(m["cum"][:, 0, :], m["next"][:, :], m["raw"]["dst"][:, :], ALU.is_lt))
            c(dve.tensor_reduce(m["cnt"][:, NEXT_OUT_OF_ORDER:NEXT_OUT_OF_ORDER + 1], m["cum"][:, 0, :], AX_X, ALU.add))
            whole, place = m["cum"][:, 0, :].bitcast(I32), m["cum"][:, 1, :]
            c(dve.tensor_scalar(whole, m["raw"]["dst"][:, :], P.bit_length() - 1, None, ALU.arith_shift_right))
            c(dve.tensor_copy(m["square"][:, :], whole))
            c(dve.tensor_scalar(whole, m["raw"]["dst"][:, :], P - 1, None, ALU.bitwise_and))
            c(dve.tensor_copy(place, whole))
            dve.wait_ge(m["w_loaded"], 16 * LOADS_W)
            c(dve.tensor_scalar(m["qscale"][:, :], m["headmask"][:, :], SCALE, None, ALU.mult))
            c(dve.tensor_scalar(m["qbias"][:, :], m["qscale"][:, :], m["w"]["bq"][:, 0:1], None, ALU.mult))
            for h in range(HEADS):
                last = dve.tensor_scalar(m["wo_heads"][:, h, :], m["w"]["Wo"][:, :], m["headmask"][:, h:h + 1], None, ALU.mult)
            last.then_inc(m["wo_masked"], 1)
            dve.wait_ge(m["wo_masked"], 1)
            dve.wait_ge(m["x_loaded"], 32)
            normalise(nc, m, dve, c, m["xres"], m["work"], m["acc"], 1)

            def one_hots(i, k):
                need(dve, m["deg_summed"], i - 1)
                for hot, keys, iota, n in ((m["hot_p"], place, m["iota_n"], P), (m["hot_t"], m["square"], m["iota_t"], NT)):
                    last = dve.tensor_tensor(hot[:, k, :, :], column(keys[:, bass.ds(i * HC, HC)], [P, HC, n]),
                                             row_of(iota[:, 0:n], [P, HC, n]), ALU.is_equal)
                last.then_inc(m["deg_hot"], 1)

            def two(i, u, r):
                one_hots(i * 2, 0)
                one_hots(i * 2 + 1, 1)
            rounds(dve, two, 0, NT // 2, 2)
            one_hots(HOT_STEPS - 1, 0)
            dve.wait_ge(m["deg_summed"], HOT_STEPS)
            dve.tensor_copy(m["cnt"][:, 0:TILES], m["bank"][7][:, 0:TILES]).then_inc(m["counted_d"], 1)
            dve.tensor_scalar(m["deg"][:, :], m["bank"][7][:, 0:NT], 1.0, None, ALU.add).then_inc(m["deg_ready"], 1)
            dve.wait_ge(m["deg_root"], 1)
            c(dve.reciprocal(m["dinv"][:, :], m["std"][:, :]))
            dve.wait_ge(m["hw_read"], NT)
            dve.tensor_tensor(m["acc"][:, :, :], m["acc"][:, :, :], column(m["dinv"][:, :], [P, NT, D]), ALU.mult).then_inc(m["g_ready"], 1)
            dve.wait_ge(m["sums_d"], 1)
            n = TILES
            ng, first, end, adj, step = (t[:, 0:n] for t in (m["ng"], m["first_d"], m["end"], m["adj"], m["step"]))
            tile_groups(dve, c, m["bank"][1][:, 0:n], GC, ng, m["ngi"][:, 0:n], first, end)
            total = m["bank"][1][:, 0:n]
            c(dve.memset(step, 0.0))
            c(dve.tensor_copy(m["tot"][:, 0:n], total))
            c(dve.tensor_tensor_scan(adj, m["tot"][:, 0:n], step, 0.0, ALU.add, ALU.add))
            c(dve.tensor_tensor(adj, adj, m["tot"][:, 0:n], ALU.subtract))
            c(dve.scalar_tensor_tensor(out=adj, in0=first, scalar=-float(GE), in1=adj, op0=ALU.mult, op1=ALU.add))
            unsorted = m["flags"][:, 0:1]
            c(dve.tensor_copy(m["flags_i"][:, :], m["bank"][1][:, NEXT_OUT_OF_ORDER:NEXT_OUT_OF_ORDER + 1]))
            c(dve.tensor_scalar(unsorted, m["bank"][1][:, NEXT_OUT_OF_ORDER:NEXT_OUT_OF_ORDER + 1], 1.0, None, ALU.min))
            c(dve.tensor_scalar(m["flags"][:, 1:2], unsorted, -1.0, 1.0, ALU.mult, ALU.add))
            c(dve.tensor_scalar(m["flags"][:, 2:3], unsorted, float(SORTED_AT), None, ALU.mult))
            c(dve.tensor_scalar(adj, adj, m["flags"][:, 1:2], m["flags"][:, 2:3], ALU.mult, ALU.add))
            c(dve.tensor_tensor(step[:, 0:n - 1], adj[:, 1:n], adj[:, 0:n - 1], ALU.subtract))
            c(dve.scalar_tensor_tensor(out=m["tot"][:, 0:n], in0=end, scalar=1.0, in1=m["ident"][:, 0:n], op0=ALU.mult, op1=ALU.mult,
                                       accum_out=m["of_tile"][:, 0:1]))
            c(dve.scalar_tensor_tensor(out=m["tot"][:, 0:n], in0=step, scalar=1.0, in1=m["ident"][:, 0:n], op0=ALU.mult, op1=ALU.mult,
                                       accum_out=m["of_tile"][:, 1:2]))
            c(dve.tensor_scalar(m["steps"][:, :], m["ones"][:, :], m["of_tile"][:, 1:2], None, ALU.mult))
            dve.tensor_scalar(m["past"][:, 0:NGD], m["iota_d"][:, :], m["of_tile"][:, 0:1], m["before"][:, n - 1:n], ALU.is_ge, ALU.mult).then_inc(m["past_ready"], 1)
            dve.wait_ge(m["past_summed"], 1)
            c(dve.tensor_scalar(m["at_f"][:, :], m["iota_d"][:, :], float(GE), adj[:, 0:1], ALU.mult, ALU.add))
            c(dve.tensor_tensor(m["at_f"][:, :], m["at_f"][:, :], m["bank"][2][:, 0:NGD], ALU.add))
            c(dve.tensor_copy(m["tile_d"][:, :], m["bank"][3][:, 0:NGD]))
            c(dve.tensor_scalar(m["flags"][:, 2:3], unsorted, float(NGD * GE + SORTED_AT), float(EDGES), ALU.mult, ALU.add))
            c(dve.tensor_scalar(m["at_d"][:, :], m["at_f"][:, :], m["flags"][:, 2:3], None, ALU.min))
            c(dve.tensor_copy(m["tile_di"][:, :], m["tile_d"][:, :]))
            c(dve.tensor_scalar(m["node_d"][:, :], m["tile_d"][:, :], float(P), None, ALU.mult))
            dve.wait_ge(m["counted_s"], COUNTS)
            c(dve.scalar_tensor_tensor(out=m["cnt_s"][:, :], in0=m["over"][:, 1:STILES + 1], scalar=-2.0, in1=m["over"][:, 0:STILES],
                                       op0=ALU.mult, op1=ALU.add))
            dve.tensor_tensor(m["cnt_s"][:, :], m["cnt_s"][:, :], m["over"][:, 2:STILES + 2], ALU.add).then_inc(m["cnt_s_ready"], 1)
            m["chain_at"] = c.n

        @block.scalar
        def _(act):
            act.wait_ge(m["w_transposed"], 1)
            nc.scalar.copy(m["wkT"][:, :], m["bank"][6][:, 0:D])
            nc.scalar.copy(m["wvT"][:, :], m["bank"][7][:, 256:256 + D])
            nc.scalar.copy(m["w_linT"][:, :], m["bank"][7][:, 0:D]).then_inc(m["wT_ready"], 1)
            act.wait_ge(m["w12_summed"], 1)
            nc.scalar.copy(m["w12"][:, :], m["bank"][7][:, 128:128 + D]).then_inc(m["w12_ready"], 1)
            act.wait_ge(m["wvo_summed"], 1)
            nc.scalar.copy(m["wvo"][:, :], m["bank"][0][:, :])
            nc.scalar.copy(m["bvo"][:, :], m["bank"][1][0:1, 0:D]).then_inc(m["wvo_ready"], 1)

            def count(b):
                nc.scalar.activation(m["row"][:, :].bitcast(F32), m["tile_of"][:, :], ACT.Relu, bias=m["one_minus_t"][:, bass.ds(b, 1)],
                                     accum_out=m["over"][:, bass.ds(b, 1)]).then_inc(m["counted_s"], 1)
                act.wait_ge(m["counted_s"], b + 1)
            act.wait_ge(m["tile_of_ready"], 1)
            with act.Fori(0, COUNTS_FIRST) as b:
                count(b)
            square_root(nc, m, act, 1)
            act.wait_ge(m["norm_ready"], 1)

            def features(i, u, r):
                b = i * COUNTS_PER_TILE + COUNTS_FIRST
                need(act, m["h_transposed"], i - 1)
                nc.scalar.activation(m["hs"][:, u, :], m["work"][:, bass.ds(i, 1), :].rearrange("p a d -> p (a d)"), ACT.Relu,
                                     scale=m["rstd"][:, bass.ds(i, 1)]).then_inc(m["h_ready"], 1)
                count(b)
                act.wait_ge(m["h_transposed"], i + 1)
                need(act, m["hw_summed"], i - 1)
                nc.scalar.copy(m["hT"][:, u, :], m["bank"][2 + u][:, 0:P]).then_inc(m["hT_ready"], 1)
                for j in range(1, COUNTS_PER_TILE):
                    count(b + j)
                act.wait_ge(m["hw_summed"], i + 1)
                nc.scalar.copy(m["acc"][:, bass.ds(i, 1), :], m["bank"][4 + u][:, 0:D].rearrange("p (a d) -> p a d", a=1)).then_inc(m["hw_read"], 1)
            rounds(act, features, 0, NT // 2, 2)
            act.wait_ge(m["deg_ready"], 1)
            nc.scalar.activation(m["std"][:, :], m["deg"][:, :], ACT.Sqrt).then_inc(m["deg_root"], 1)
            with act.Fori(COUNTS_LAST, COUNTS) as b:
                count(b)

        @block.tensor
        def _(pe):
            pe.wait_ge(m["consts"], 1)
            pe.wait_ge(m["w_loaded"], 16 * LOADS_W)
            pe.transpose(m["bank"][6][:, 0:D], m["w"]["Wk"][:, :], m["ident"][:, :])
            pe.transpose(m["bank"][7][:, 256:256 + D], m["w"]["Wv"][:, :], m["ident"][:, :])
            pe.transpose(m["bank"][7][:, 0:D], m["w"]["W_lin"][:, :], m["ident"][:, :]).then_inc(m["w_transposed"], 1)
            pe.wait_ge(m["wT_ready"], 1)
            pe.matmul(m["bank"][7][:, 128:128 + D], m["w_linT"][:, :], m["w"]["W_gcn"][:, :], start=True, stop=True).then_inc(m["w12_summed"], 1)
            pe.wait_ge(m["wo_masked"], 1)
            pe.matmul(m["bank"][0][:, :], m["wvT"][:, :], m["wo_heads"][:, :, :].rearrange("p h d -> p (h d)"), start=True, stop=True)
            pe.matmul(m["bank"][1][0:1, 0:D], m["w"]["bv"][:, 0:1], m["w"]["Wo"][:, :], start=True, stop=True).then_inc(m["wvo_summed"], 1)
            pe.wait_ge(m["w12_ready"], 1)

            def degrees(i, k):
                pe.wait_ge(m["deg_hot"], i + 1)
                for j in range(HC):
                    last = pe.matmul(m["bank"][7][:, 0:NT], m["hot_p"][:, k, j, :], m["hot_t"][:, k, j, :], start=zero(i) and j == 0, stop=True,
                                     skip_group_check=True)
                last.then_inc(m["deg_summed"], 1)

            def features(i, u, r):
                pe.wait_ge(m["h_ready"], i + 1)
                need(pe, m["hT_ready"], i - 1)
                pe.transpose(m["bank"][2 + u][:, 0:P], m["hs"][:, u, :], m["ident"][:, :]).then_inc(m["h_transposed"], 1)
                degrees(i * 2, 0)
                pe.wait_ge(m["hT_ready"], i + 1)
                need(pe, m["hw_read"], i - 1)
                pe.matmul(m["bank"][4 + u][:, 0:D], m["hT"][:, u, :], m["w12"][:, :], start=True, stop=True).then_inc(m["hw_summed"], 1)
                degrees(i * 2 + 1, 1)
            rounds(pe, features, 0, NT // 2, 2)
            degrees(HOT_STEPS - 1, 0)
            pe.wait_ge(m["wvo_ready"], 1)
            pe.wait_ge(m["counted_d"], 1)
            pe.matmul(m["bank"][1][:, 0:64], m["ones"][:, :], m["cnt"][:, :], start=True, stop=True).then_inc(m["sums_d"], 1)
            pe.wait_ge(m["past_ready"], 1)
            pe.matmul(m["bank"][2][:, 0:NGD], m["steps"][:, :], m["past"][:, 0:NGD], start=True, stop=True)
            pe.matmul(m["bank"][3][:, 0:NGD], m["ones"][:, :], m["past"][:, 0:NGD], start=True, stop=True).then_inc(m["past_summed"], 1)
            pe.wait_ge(m["cnt_s_ready"], 1)
            pe.wait_ge(m["hw_read"], NT)
            pe.matmul(m["bank"][4][:, 0:STILES], m["before"][:, :], m["cnt_s"][:, :], start=True, stop=True)
            pe.matmul(m["bank"][5][:, 0:STILES], m["ones"][:, :], m["cnt_s"][:, :], start=True, stop=True).then_inc(m["sums_s"], 1)



def scatter(nc, m, pool, table, staged, scattered):
    def body(i, u, r):
        apart(m, pool, staged[u], r * 32 + 32)
        for j in range(SC):
            pool.indirect_dma_start(out=table, out_offset=bass.IndirectOffsetOnAxis(ap=m["row_st"][:, u, j:j + 1], axis=0),
                                    in_=m["pair_st"][:, u, j, :], in_offset=None).then_inc(scattered[u], 16)
    rounds(pool, body, 0, COLS // SC // 2, 2)
    for u in range(2):
        pool.wait_ge(scattered[u], COLS // 2 * 16)


def stage(nc, m, sp, staged, scattered):
    def body(i, u, r):
        apart(m, sp, scattered[u], r * (16 * SC))
        sp.dma_start(m["row_st"][:, u, :], m["row"][:, bass.ds(i * SC, SC)]).then_inc(staged[u], 16)
        sp.dma_start(m["pair_st"][:, u, :, :], m["pairs"][:, bass.ds(i * SC, SC), :]).then_inc(staged[u], 16)
    rounds(sp, body, 0, COLS // SC // 2, 2)


def out_of_order(m, eng):
    return eng.value_load(m["flags_i"][0:1, 0:1], min_val=0, max_val=E)


def unsorted_block(nc, m):
    with nc.Block() as block:
        @block.sync
        def _(sp):
            with sp.If(out_of_order(m, sp) > 0):
                t3 = in_partitions(m["table_d"][SORTED_AT:SORTED_AT + NGD * GE, :])
                for j in range(0, NGD * GC, EMPTY):
                    n = min(EMPTY, NGD * GC - j)
                    sp.dma_start(t3[:, j:j + n, :], m["empty"][:, 0:n, :]).then_inc(m["emptied_d"], 16)
                sp.wait_ge(m["emptied_d"], 16 * -(-NGD * GC // EMPTY))
                sp.wait_ge(m["rows_d"], 1)
                stage(nc, m, sp, m["staged_d"], m["scattered_d"])

        @block.gpsimd
        def _(pool):
            with pool.If(out_of_order(m, pool) > 0):
                pool.iota(m["row"][:, :].bitcast(F32), [[1, COLS]], base=SORTED_AT + NGD * GE + 1, channel_multiplier=0,
                          allow_small_or_imprecise_dtypes=True).then_inc(m["junk_d"], 1)
                scatter(nc, m, pool, m["table_d"], m["staged_d"], m["scattered_d"])

        @block.vector
        def _(dve):
            with dve.If(out_of_order(m, dve) > 0):
                c = Chain(dve, m["unsorted_chain"])
                mask, cum, pos = m["mask"][:, 0, :], m["cum"][:, 0, :], m["cum"][:, 1, :]
                dve.wait_ge(m["junk_d"], 1)
                with dve.Fori(0, TILES) as b:
                    dve.tensor_scalar(mask, m["square"][:, :], m["iota_t"][:, bass.ds(b, 1)], 0.0, ALU.is_equal, ALU.add,
                                      accum_out=m["cnt"][:, bass.ds(b, 1)]).then_inc(m["part_counted"], 1)
                    dve.wait_ge(m["part_counted"], b + 1)
                dve.wait_ge(m["part_summed"], 1)
                c(dve.tensor_scalar(m["base_d"][:, 0:TILES], m["first_d"][:, 0:TILES], float(GE), float(SORTED_AT), ALU.mult, ALU.add))
                c(dve.tensor_tensor(m["base_d"][:, 0:TILES], m["base_d"][:, 0:TILES], m["bank"][0][:, 0:TILES], ALU.add))
                c(dve.scalar_tensor_tensor(out=pos, in0=m["square"][:, :], scalar=float(TILES), in1=m["row"][:, :].bitcast(F32),
                                           op0=ALU.is_ge, op1=ALU.mult))
                with dve.Fori(0, TILES) as b:
                    dve.tensor_scalar(mask, m["square"][:, :], m["iota_t"][:, bass.ds(b, 1)], None, ALU.is_equal).then_inc(m["placed_d"], 1)
                    dve.wait_ge(m["placed_d"], b * 4 + 1)
                    dve.tensor_tensor_scan(cum, mask, mask, m["base_d"][:, bass.ds(b, 1)], ALU.add, ALU.max).then_inc(m["placed_d"], 1)
                    dve.wait_ge(m["placed_d"], b * 4 + 2)
                    dve.tensor_tensor(cum, cum, mask, ALU.mult).then_inc(m["placed_d"], 1)
                    dve.wait_ge(m["placed_d"], b * 4 + 3)
                    dve.tensor_tensor(pos, pos, cum, ALU.add).then_inc(m["placed_d"], 1)
                    dve.wait_ge(m["placed_d"], b * 4 + 4)
                dve.tensor_scalar(m["row"][:, :], pos, -1.0, None, ALU.add).then_inc(m["rows_d"], 1)


        @block.tensor
        def _(pe):
            with pe.If(out_of_order(m, pe) > 0):
                pe.wait_ge(m["part_counted"], TILES)
                pe.matmul(m["bank"][0][:, 0:TILES], m["before"][:, :], m["cnt"][:, 0:TILES], start=True, stop=True).then_inc(m["part_summed"], 1)



def layer0_slots(nc, m, i):
    at, = registers(nc, mybir.EngineType.SP, (m["at_d"][0:1, bass.ds(i, 1)], SORTED_AT + (NGD - 1) * GE))
    return in_partitions(m["table_d"][bass.ds(at, GE), :])


def one_hot(dve, out, iota, keys, first_node, shape, compare=ALU.is_equal):
    return dve.scalar_tensor_tensor(out=out, in0=keys.to_broadcast(shape), scalar=first_node, in1=iota.to_broadcast(shape),
                                    op0=ALU.subtract, op1=compare)


def gather(m, pool, rows, source, u, gathered):
    for j in range(GC):
        pool.indirect_dma_start(out=rows[:, u, j, :], out_offset=None, in_=source,
                                in_offset=bass.IndirectOffsetOnAxis(ap=m["tab"][:, u, j, 0:1], axis=0)).then_inc(gathered[u], 16)


def layer0_block(nc, m):
    placing = STILES // PLACED_PER_ROUND
    every = RING // PLACED_PER_ROUND


    with nc.Block() as block:
        @block.sync
        def _(sp):
            def body(i, u, r):
                slots = layer0_slots(nc, m, i)
                apart(m, sp, m["l0_hot"], i - (RING - 1))
                apart(m, sp, m["l0_gathered"][u], r * (16 * GC))
                sp.dma_start(m["tab"][:, u, :, :], slots).then_inc(m["l0_tab"][u], 16)
            rounds(sp, body, 0, NGD // RING, RING)

        @block.gpsimd
        def _(pool):
            pool.iota(m["row"][:, :].bitcast(F32), [[1, COLS]], base=NGS * SGE + 1, channel_multiplier=0,
                      allow_small_or_imprecise_dtypes=True)
            pool.iota(m["pairs"][:, :, 0:1].rearrange("p j a -> p (j a)"), [[1, COLS]], base=0, channel_multiplier=COLS).then_inc(m["junk_s"], 1)

            def body(i, u, r):
                need(pool, m["l0_summed"], i - (RING - 1))
                apart(m, pool, m["l0_tab"][u], r * 16 + 16)
                gather(m, pool, m["g_rows"], m["g_dram"], u, m["l0_gathered"])
            rounds(pool, body, 0, NGD // RING, RING)

        @block.scalar
        def _(act):
            def masks(b, k, r):
                need(act, m["mask_ready"], b)
                need(act, m["masked"], b - (PLACED_PER_ROUND - 1))
                nc.scalar.activation(m["square"][:, :], m["tile_of"][:, :], ACT.Square, bias=m["minus_t"][:, bass.ds(b, 1)]).then_inc(m["squared_p"], 1)
                act.wait_ge(m["squared_p"], b + 1)
                nc.scalar.activation(m["mask"][:, k, :], m["square"][:, :], ACT.Relu, bias=m["ones"][:, 0:1], scale=-1.0).then_inc(m["mask_ready"], 1)
            rounds(act, masks, 0, placing, PLACED_PER_ROUND)

        @block.tensor
        def _(pe):
            def group(i, u, r):
                pe.wait_ge(m["l0_hot"], i + 1)
                pe.wait_ge(m["l0_gathered"][u], r * (16 * GC) + 16 * GC)
                need(pe, m["l0_added"], i - (RING - 1))
                for j in range(GC):
                    last = pe.matmul(m["bank"][u][:, 0:D], m["hot"][:, u, j, :], m["g_rows"][:, u, j, :], start=(j == 0), stop=(j == GC - 1))
                last.then_inc(m["l0_summed"], 1)

            def place(b, k, r):
                pe.wait_ge(m["masked"], b + 1)
                for j in range(BANKS):
                    last = pe.matmul(m["bank"][4 + j][:, 0:BANK_COLS], m["ident"][:, :], m["cum"][:, k, j * BANK_COLS:(j + 1) * BANK_COLS],
                                     start=zero(b), stop=True, skip_group_check=True)
                last.then_inc(m["placed"], 1)
            def both(i, u, r):
                group(i, u, r)
                if u % every == 0 and not zero(i):
                    k = (u // every - 1) % PLACED_PER_ROUND
                    place(r * PLACED_PER_ROUND + u // every - 1, k, r)
            pe.wait_ge(m["base_ready"], 1)
            rounds(pe, both, 0, placing, RING)
            place(STILES - 1, PLACED_PER_ROUND - 1, placing)
            rounds(pe, group, placing, NGD // RING, RING)

        @block.vector
        def _(dve):
            c = Chain(dve, m["dve_chain"], m["chain_at"])
            n = STILES
            tile_groups(dve, c, m["bank"][5][:, 0:n], SGC, m["past"][:, 0:n], m["ngi"][:, 0:n], m["first_s"][:, :], m["end_s"][:, :])
            c(dve.tensor_copy(m["used_i"][:, :], m["end_s"][:, n - 1:n]))
            c(dve.tensor_scalar(m["base_s"][:, :], m["first_s"][:, :], float(SGE), None, ALU.mult))
            dve.tensor_tensor(m["base_s"][:, :], m["base_s"][:, :], m["bank"][4][:, 0:n], ALU.add).then_inc(m["base_ready"], 1)
            dve.wait_ge(m["base_ready"], 1)

            tiles = {}

            def load_tiles(first, n):
                return registers(nc, mybir.EngineType.DVE, (m["tile_di"][0:1, bass.ds(first, n)], TILES - 1))

            def add(i, u, t):
                dve.wait_ge(m["l0_summed"], i + 1)
                need(dve, m["l0_added"], i)
                dve.tensor_tensor(m["acc"][:, bass.ds(t, 1), :], m["acc"][:, bass.ds(t, 1), :],
                                  row_of(m["bank"][u][:, 0:D], [P, 1, D]), ALU.add).then_inc(m["l0_added"], 1)

            def hot(i, u, r):
                dve.wait_ge(m["l0_tab"][u], r * 16 + 16)
                need(dve, m["l0_summed"], i - (RING - 1))
                one_hot(dve, m["hot"][:, u, :, :], row_of(m["iota_n"][:, :], [P, 1, P]), m["tab"][:, u, :, 1:2],
                        m["node_d"][:, bass.ds(i, 1)], [P, GC, P]).then_inc(m["l0_hot"], 1)

            def group(i, u, r):
                if not (isinstance(i, int) and i == NGD - 1):
                    hot(i + 1, (u + 1) % RING, r if u < RING - 1 else r + 1)
                if zero(i):
                    tiles.update(enumerate(load_tiles(0, RING - 1), 1))
                elif u == 0:
                    tiles.update(enumerate(load_tiles(i - 1, RING)))
                if not zero(i):
                    add(i - 1, (u - 1) % RING, tiles[u])

            def place(b, k, r):
                dve.wait_ge(m["mask_ready"], b + 1)
                need(dve, m["placed"], b - (PLACED_PER_ROUND - 1))
                dve.tensor_tensor_scan(m["cum"][:, k, :], m["mask"][:, k, :], m["mask"][:, k, :], m["base_s"][:, bass.ds(b, 1)],
                                       ALU.add, ALU.max).then_inc(m["scanned"], 1)
                dve.wait_ge(m["scanned"], b + 1)
                dve.tensor_tensor(m["cum"][:, k, :], m["cum"][:, k, :], m["mask"][:, k, :], ALU.mult).then_inc(m["masked"], 1)
            def both(i, u, r):
                group(i, u, r)
                if u % every == every - 1:
                    k = u // every
                    place(r * PLACED_PER_ROUND + k, k, r)
            hot(0, 0, 0)
            rounds(dve, both, 0, placing, RING)
            rounds(dve, group, placing, NGD // RING - 1, RING)
            for u in range(RING):
                group(NGD - RING + u, u, NGD // RING - 1)
            add(NGD - 1, RING - 1, load_tiles(NGD - 1, 1)[0])
            dve.wait_ge(m["l0_added"], NGD)
            dve.wait_ge(m["placed"], STILES)
            dve.wait_ge(m["junk_s"], 1)
            c(dve.tensor_copy(m["pairs"][:, :, 1:2], m["raw"]["src"][:, :].rearrange("p (j a) -> p j a", a=1)))
            c(dve.scalar_tensor_tensor(out=m["cum"][:, 0, :], in0=m["tile_of"][:, :], scalar=float(STILES), in1=m["row"][:, :].bitcast(F32),
                                       op0=ALU.is_ge, op1=ALU.mult))
            for j in range(BANKS):
                at = slice(j * BANK_COLS, (j + 1) * BANK_COLS)
                c(dve.tensor_tensor(m["cum"][:, 0, at], m["cum"][:, 0, at], m["bank"][4 + j][:, 0:BANK_COLS], ALU.add))
            c(dve.tensor_scalar(m["row"][:, :], m["cum"][:, 0, :], -1.0, None, ALU.add))
            m["chain_at"] = c.n



def nodes_block(nc, m):
    with nc.Block() as block:
        @block.gpsimd
        def _(pool):
            scatter(nc, m, pool, m["table_s"], m["staged_s"], m["scattered_s"])

        @block.sync
        def _(sp):
            stage(nc, m, sp, m["staged_s"], m["scattered_s"])

        @block.vector
        def _(dve):
            c = Chain(dve, m["dve_chain"], m["chain_at"])
            shape = [P, NT, D]

            def row(n):
                return row_of(m["w"][n][:, :], shape)
            c(dve.tensor_tensor(m["acc"][:, :, :], m["acc"][:, :, :], column(m["dinv"][:, :], shape), ALU.mult))
            c(dve.tensor_tensor(m["acc"][:, :, :], m["acc"][:, :, :], row("b_gcn"), ALU.add))
            normalise(nc, m, dve, c, m["acc"], m["work"], m["acc"], 2)
            c(dve.tensor_tensor(m["work"][:, :, :], m["work"][:, :, :], column(m["rstd"][:, :], shape), ALU.mult))
            c(dve.tensor_tensor(m["work"][:, :, :], m["work"][:, :, :], row("gamma"), ALU.mult))
            c(dve.tensor_tensor(m["work"][:, :, :], m["work"][:, :, :], row("beta"), ALU.add))
            c(dve.scalar_tensor_tensor(out=m["xres"][:, :, :], in0=m["work"][:, :, :], scalar=0.0, in1=m["xres"][:, :, :], op0=ALU.max, op1=ALU.add))
            normalise(nc, m, dve, c, m["xres"], m["work"], m["acc"], 3)

            def normal(i, u, r):
                need(dve, m["h2_transposed"], i - 1)
                dve.tensor_scalar(m["hs"][:, u, :], m["work"][:, bass.ds(i, 1), :], m["rstd"][:, bass.ds(i, 1)], 0.0, ALU.mult,
                                  ALU.max).then_inc(m["h2_ready"], 1)
            rounds(dve, normal, 0, NT // 2, 2)
            c(dve.memset(m["mx"][:, :], FLOOR))
            c(dve.tensor_tensor(m["xres"][:, :, :], m["xres"][:, :, :], row("bo"), ALU.add))
            c(dve.memset(m["tile_s"][:, :], 0.0))
            with dve.Fori(0, STILES - 1) as b:
                dve.scalar_tensor_tensor(out=m["tile_s"][:, :], in0=m["iota_s"][:, :], scalar=m["end_s"][:, bass.ds(b, 1)], in1=m["tile_s"][:, :],
                                         op0=ALU.is_ge, op1=ALU.add).then_inc(m["stepped_s"], 1)
                dve.wait_ge(m["stepped_s"], b + 1)
            c(dve.tensor_copy(m["tile_si"][:, :], m["tile_s"][:, :]))
            c(dve.tensor_scalar(m["node_s"][:, :], m["tile_s"][:, :], float(SN), None, ALU.mult))
            m["chain_at"] = c.n

        @block.scalar
        def _(act):
            square_root(nc, m, act, 2)
            square_root(nc, m, act, 3)

            def copies(i, u, r):
                act.wait_ge(m["h2_transposed"], i + 1)
                need(act, m["q_summed"], i - 1)
                nc.scalar.copy(m["hT"][:, u, :], m["bank"][u][:, 0:P]).then_inc(m["h2T_ready"], 1)
                act.wait_ge(m["q_summed"], i + 1)
                need(act, m["G_summed"], i - 1)
                for h in range(HEADS):
                    last = nc.scalar.activation(m["qm"][:, u, :, h, :], m["bank"][2 + u][:, 0:P].rearrange("d (q n) -> d q n", q=PARTS),
                                                ACT.Identity, bias=m["qbias"][:, h:h + 1], scale=m["qscale"][:, h:h + 1])
                last.then_inc(m["q_ready"], 1)
                act.wait_ge(m["G_summed"], i + 1)
                need(act, m["G_stored"][u], r * 16)
                nc.scalar.copy(m["gst"][:, u, :, 0:P], m["bank"][4 + u][:, :].rearrange("d (q n) -> d q n", q=PARTS)).then_inc(m["G_copied"], 1)
                nc.scalar.copy(m["gst"][:, u, :, P:P + 1], m["bank"][6 + u][:, 0:PARTS].rearrange("d (q n) -> d q n", n=1)).then_inc(m["G_ready"], 1)
                apart(m, act, m["G_copied"], i + 1)
                apart(m, act, m["G_ready"], i + 1)
                act.dma_start(m["G_dram"][bass.ds(i * (PARTS * P), PARTS * P), :].rearrange("(q d) n -> d q n", q=PARTS),
                              m["gst"][:, u, :, :]).then_inc(m["G_stored"][u], 16)
            rounds(act, copies, 0, NT // 2, 2)
            for u in range(2):
                act.wait_ge(m["G_stored"][u], NT // 2 * 16)

        @block.tensor
        def _(pe):
            def body(i, u, r):
                pe.wait_ge(m["h2_ready"], i + 1)
                need(pe, m["h2T_ready"], i - 1)
                pe.transpose(m["bank"][u][:, 0:P], m["hs"][:, u, :], m["ident"][:, :]).then_inc(m["h2_transposed"], 1)
                pe.wait_ge(m["h2T_ready"], i + 1)
                need(pe, m["q_ready"], i - 1)
                pe.matmul(m["bank"][2 + u][:, 0:P], m["w"]["Wq"][:, :], m["hT"][:, u, :], start=True, stop=True).then_inc(m["q_summed"], 1)
                pe.wait_ge(m["q_ready"], i + 1)
                need(pe, m["G_ready"], i - 1)
                q = m["qm"][:, u, :, :, :].rearrange("d q h n -> d (q h n)")
                pe.matmul(m["bank"][4 + u][:, :], m["wkT"][:, :], q, start=True, stop=True)
                for j in range(PARTS):
                    last = pe.matmul(m["bank"][6 + u][:, j:j + 1], q[:, j * P:(j + 1) * P], m["w"]["bk"][:, 0:1], start=True, stop=True)
                last.then_inc(m["G_summed"], 1)
            rounds(pe, body, 0, NT // 2, 2)



def layer1_block(nc, m):
    trK, scores, trE, sums = m["bank"][0:2], m["bank"][2:4], m["bank"][4:6], m["bank"][6:8]
    usual, all_of_them = USUAL // SRING, NGS // SRING

    def group_tiles(engine, first, n):
        return registers(nc, engine, (m["tile_si"][0:1, bass.ds(first, n)], STILES - 1))

    def twice(eng, part):
        part(0, usual)
        with eng.If(eng.value_load(m["used_i"][0:1, 0:1], min_val=0, max_val=NGS) > USUAL):
            part(usual, all_of_them)

    def before(i, lag, first):
        return isinstance(i, int) and i < first * SRING + lag

    def ring(u):
        return u % SRING

    with nc.Block() as block:
        @block.sync
        def _(sp):
            def body(i, u, r):
                apart(m, sp, m["l1_hot"], i - (SRING - 1))
                apart(m, sp, m["l1_gathered"][u], r * (16 * SGC))
                sp.dma_start(m["tab_s"][:, u, :, :], in_partitions(m["table_s"][bass.ds(i * SGE, SGE), :])).then_inc(m["l1_tab"][u], 16)
                t, = group_tiles(mybir.EngineType.SP, i, 1)
                apart(m, sp, m["max_ready"], i - (SRING - 1))
                sp.dma_start(m["G"][:, u, :], m["G_dram"][bass.ds(t * P, P), :]).then_inc(m["G_loaded"][u], 16)
            twice(sp, lambda first, last: steps(sp, body, first, last, SRING))

        @block.gpsimd
        def _(pool):
            pool.memset(m["agg"][:, :, :], 0.0)
            pool.memset(m["kv_rows"][:, :, :, 2 * D:], 1.0).then_inc(m["rows_ready"], 1)

            def body(i, u, r):
                need(pool, m["l1_summed"], i - (SRING - 1))
                apart(m, pool, m["l1_tab"][u], r * 16 + 16)
                for j in range(SGC):
                    pool.indirect_dma_start(out=m["kv_rows"][:, u, j, 0:2 * D], out_offset=None, in_=m["kv"],
                                            in_offset=bass.IndirectOffsetOnAxis(ap=m["tab_s"][:, u, j, 0:1], axis=0)).then_inc(m["l1_gathered"][u], 16)
            twice(pool, lambda first, last: steps(pool, body, first, last, SRING))

        @block.tensor
        def _(pe):
            def score(i, u, r):
                k = u % 2
                pe.wait_ge(m["l1_hot"], i + 1)
                need(pe, m["exp_ready"], i - 1)
                for j in range(SGC):
                    pe.matmul(scores[k][:, j * P:(j + 1) * P], m["others"][:, u, j, :], m["out_b"][:, :], start=(j == 0), stop=False, skip_group_check=True)
                pe.wait_ge(m["kT_ready"], i + 1)
                pe.wait_ge(m["G_loaded"][u], r * 16 + 16)
                pe.matmul(scores[k][:, 0:SGE], m["G"][:, u, 0:P], m["kT"][:, k, :], start=False, stop=True, skip_group_check=True).then_inc(m["scored"], 1)

            def keys(i, u, r):
                pe.wait_ge(m["l1_gathered"][u], r * (16 * SGC) + 16 * SGC)
                need(pe, m["kT_ready"], i - 1)
                for j in range(SGC):
                    last = pe.transpose(trK[u % 2][:, j * P:(j + 1) * P], m["kv_rows"][:, u, j, 0:D], m["ident"][:, :])
                last.then_inc(m["k_transposed"], 1)

            def weights(i, u):
                pe.wait_ge(m["exp_ready"], i + 1)
                need(pe, m["eT_ready"], i - 1)
                for j in range(SGC):
                    last = pe.transpose(trE[u % 2][:, j * P:(j + 1) * P], m["ex"][:, u % 2, j * P:(j + 1) * P], m["ident"][:, :])
                last.then_inc(m["e_transposed"], 1)

            def add_up(i, u):
                pe.wait_ge(m["eT_ready"], i + 1)
                need(pe, m["l1_added"], i - 1)
                for j in range(SGC):
                    last = pe.matmul(sums[u % 2][:, 0:VW], m["exT"][:, u % 2, j * P:(j + 1) * P], m["kv_rows"][:, u, j, D:D + VW],
                                     start=(j == 0), stop=(j == SGC - 1))
                last.then_inc(m["l1_summed"], 1)

            def part(first, last):
                end = last * SRING

                def body(i, u, r):
                    score(i, u, r)
                    if not (isinstance(i, int) and i == end - 1):
                        keys(i + 1, ring(u + 1), r if u < SRING - 1 else r + 1)
                    if not before(i, 1, first):
                        weights(i - 1, ring(u - 1))
                    if not before(i, 2, first):
                        add_up(i - 2, ring(u - 2))
                keys(first * SRING, 0, first)
                steps(pe, body, first, last, SRING)
                weights(end - 1, SRING - 1)
                add_up(end - 2, SRING - 2)
                add_up(end - 1, SRING - 1)
            pe.wait_ge(m["rows_ready"], 1)
            twice(pe, part)

        @block.scalar
        def _(act):
            def keys(i, u):
                act.wait_ge(m["k_transposed"], i + 1)
                need(act, m["scored"], i - 1)
                nc.scalar.copy(m["kT"][:, u % 2, :], trK[u % 2][:, 0:SGE]).then_inc(m["kT_ready"], 1)

            def weights(i, u):
                act.wait_ge(m["e_transposed"], i + 1)
                need(act, m["l1_summed"], i - 1)
                nc.scalar.copy(m["exT"][:, u % 2, :], trE[u % 2][:, 0:SGE]).then_inc(m["eT_ready"], 1)

            def exponentials(i, u):
                act.wait_ge(m["max_ready"], i + 1)
                need(act, m["l1_added"], i - (SRING - 1))
                nc.scalar.activation(m["decay"][:, u:u + 1], m["drop"][:, u:u + 1], ACT.Exp).then_inc(m["decay_ready"], 1)
                need(act, m["e_transposed"], i - 1)
                nc.scalar.activation(m["ex"][:, u % 2, :], scores[u % 2][:, 0:SGE], ACT.Exp, bias=m["shift"][:, u:u + 1]).then_inc(m["exp_ready"], 1)

            def part(first, last):
                end = last * SRING

                def body(i, u, r):
                    if not (isinstance(i, int) and i == end - 1):
                        keys(i + 1, ring(u + 1))
                    if not before(i, 1, first):
                        weights(i - 1, ring(u - 1))
                    exponentials(i, u)
                keys(first * SRING, 0)
                steps(act, body, first, last, SRING)
                weights(end - 1, SRING - 1)
            twice(act, part)

        @block.vector
        def _(dve):
            tiles = {}

            def hot(i, u, r):
                dve.wait_ge(m["l1_tab"][u], r * 16 + 16)
                need(dve, m["scored"], i - (SRING - 1))
                one_hot(dve, m["others"][:, u, :, :], row_of(m["iota_h"][:, :], [P, 1, P]), m["tab_s"][:, u, :, 1:2],
                        m["node_s"][:, bass.ds(i, 1)], [P, SGC, P], ALU.not_equal).then_inc(m["l1_hot"], 1)

            def maxima(i, u, r, t):
                at = slice(u, u + 1)
                need(dve, m["exp_ready"], i - (SRING - 1))
                apart(m, dve, m["scored"], i + 1)
                dve.tensor_reduce(m["gmax"][:, at], scores[u % 2][:, 0:SGE], AX_X, ALU.max).then_inc(m["reduced"], 1)
                c, mx = m["G"][:, u, P:P + 1], m["mx"][:, bass.ds(t, 1)]
                dve.wait_ge(m["G_loaded"][u], r * 16 + 16)
                need(dve, m["max_ready"], i)
                dve.wait_ge(m["reduced"], i + 1)
                dve.scalar_tensor_tensor(out=m["mnew"][:, at], in0=m["gmax"][:, at], scalar=c, in1=mx, op0=ALU.add,
                                         op1=ALU.max).then_inc(m["maxing"], 1)
                dve.wait_ge(m["maxing"], i + 1)
                dve.tensor_tensor(m["drop"][:, at], mx, m["mnew"][:, at], ALU.subtract).then_inc(m["dropped"], 1)
                dve.tensor_tensor(m["shift"][:, at], c, m["mnew"][:, at], ALU.subtract).then_inc(m["shifted"], 1)
                dve.wait_ge(m["dropped"], i + 1)
                dve.scalar_tensor_tensor(out=mx, in0=m["gmax"][:, at], scalar=c, in1=mx, op0=ALU.add,
                                         op1=ALU.max).then_inc(m["max_ready"], 1)

            def add(i, u, t):
                dve.wait_ge(m["decay_ready"], i + 1)
                need(dve, m["l1_added"], i)
                dve.wait_ge(m["l1_summed"], i + 1)
                agg = m["agg"][:, bass.ds(t, 1), :]
                dve.scalar_tensor_tensor(out=agg, in0=agg, scalar=m["decay"][:, u:u + 1], in1=row_of(sums[u % 2][:, 0:VW], [P, 1, VW]),
                                         op0=ALU.mult, op1=ALU.add).then_inc(m["l1_added"], 1)

            def part(first, last):
                end = last * SRING

                def body(i, u, r):
                    if u == 0 and before(i, 2, first):
                        tiles.update(enumerate(group_tiles(mybir.EngineType.DVE, i, SRING)))
                    elif u == 0:
                        tiles.update(enumerate(group_tiles(mybir.EngineType.DVE, i - 2, SRING + 2), -2))
                    maxima(i, u, r, tiles[u])
                    if not (isinstance(i, int) and i >= end - 2):
                        hot(i + 2, ring(u + 2), r if u < SRING - 2 else r + 1)
                    if not before(i, 2, first):
                        add(i - 2, ring(u - 2), tiles[u - 2])
                hot(first * SRING, 0, first)
                hot(first * SRING + 1, 1, first)
                steps(dve, body, first, last, SRING)
                add(end - 2, SRING - 2, tiles[SRING - 2])
                add(end - 1, SRING - 1, tiles[SRING - 1])
                dve.wait_ge(m["l1_added"], end)
            dve.wait_ge(m["rows_ready"], 1)
            twice(dve, part)


def output_block(nc, m):
    trA, outs, trH = m["bank"][0:2], m["bank"][2:4], m["bank"][4:6]

    def tiles_of_nodes(eng, body):
        for i in range(3):
            body(i, i % 2)
        with eng.Fori(1, TILES // 2) as r:
            body(r * 2 + 1, 1)
            body(r * 2 + 2, 0)

    with nc.Block() as block:
        @block.vector
        def _(dve):
            c = Chain(dve, m["dve_chain"], m["chain_at"])
            c(dve.tensor_scalar(m["rl"][:, :], m["agg"][:, :, D:VW].rearrange("p t a -> p (t a)"), 0.5, None, ALU.max))
            c(dve.reciprocal(m["rl"][:, :], m["rl"][:, :]))

            def own(i, u):
                need(dve, m["a_transposed"], i - 1)
                dve.tensor_tensor(m["y"][:, u, :, :], m["agg"][:, bass.ds(i * PARTS, PARTS), :],
                                  column(m["rl"][:, bass.ds(i * PARTS, PARTS)], [P, PARTS, VW]), ALU.mult).then_inc(m["y_ready"], 1)
                if not (isinstance(i, int) and i < 2):
                    add(i - 2, u)

            def add(i, u):
                dve.wait_ge(m["o_summed"], i + 1)
                xr = m["xres"][:, bass.ds(i, 1), :]
                dve.tensor_tensor(xr, xr, row_of(outs[u][:, 0:D], [P, 1, D]), ALU.add).then_inc(m["o_added"], 1)
            tiles_of_nodes(dve, own)
            add(TILES - 2, 1)
            add(TILES - 1, 0)

        @block.scalar
        def _(act):
            def copies(i, u):
                act.wait_ge(m["a_transposed"], i + 1)
                need(act, m["o_summed"], i - 1)
                for h in range(HEADS):
                    nc.scalar.copy(m["aT"][:, u, h, :].rearrange("d (q n) -> d q n", q=PARTS),
                                   trA[u][:, :].rearrange("d (q g n) -> d q g n", q=PARTS, g=HEADS)[:, :, h, :])
                nc.scalar.copy(m["has"][:, u, :], trH[u][0:1, 0:P]).then_inc(m["aT_ready"], 1)
            tiles_of_nodes(act, copies)

        @block.tensor
        def _(pe):
            def body(i, u):
                pe.wait_ge(m["y_ready"], i + 1)
                need(pe, m["aT_ready"], i - 1)
                for q in range(PARTS):
                    pe.transpose(trA[u][:, q * P:(q + 1) * P], m["y"][:, u, q, 0:D], m["ident"][:, :])
                    last = pe.matmul(trH[u][0:1, q * SN:(q + 1) * SN], m["y"][:, u, q, D:VW], m["ident"][:, 0:SN], start=True, stop=True)
                last.then_inc(m["a_transposed"], 1)
                if not zero(i):
                    outputs(i - 1, 1 - u)

            def outputs(i, u):
                pe.wait_ge(m["aT_ready"], i + 1)
                need(pe, m["o_added"], i - 1)
                for h in range(HEADS):
                    pe.matmul(outs[u][:, 0:D], m["aT"][:, u, h, :], m["wvo"][:, h * D:(h + 1) * D], start=(h == 0), stop=False)
                pe.matmul(outs[u][:, 0:D], m["has"][:, u, :], m["bvo"][:, :], start=False, stop=True).then_inc(m["o_summed"], 1)
            tiles_of_nodes(pe, body)
            outputs(TILES - 1, 0)

        @block.sync
        def _(sp):
            sp.wait_ge(m["o_added"], TILES)
            sp.dma_start(node_tiles(m["out"][0:N // P * P, :]), m["xres"][:, 0:N // P, :]).then_inc(m["out_stored"], 16)
            sp.dma_start(m["out"][N // P * P:N, :], m["xres"][0:N % P, N // P, :]).then_inc(m["out_stored"], 16)
            sp.wait_ge(m["out_stored"], 32)


SEMAPHORES = """
    held paddings consts keys_loaded x_loaded w_loaded emptied emptied_d pool_chain dve_chain unsorted_chain
    sqrt_asked sqrt_done pairs_ready pairs_stored counted_d sums_d w_transposed wT_ready w12_summed w12_ready
    h_ready h_transposed hT_ready hw_summed hw_read junk_d placed_d rows_d
    deg_hot deg_summed deg_ready deg_root g_ready g_stored counted_s cnt_s_ready sums_s tile_of_ready norm_ready
    past_ready past_summed part_counted part_summed
    l0_hot l0_summed l0_added junk_s squared_p mask_ready scanned masked placed base_ready
    h2_ready h2_transposed h2T_ready q_summed q_ready G_summed G_copied G_ready stepped_s
    wo_masked wvo_summed wvo_ready rows_ready l1_hot k_transposed kT_ready scored reduced maxing dropped shifted max_ready
    decay_ready exp_ready e_transposed eT_ready l1_summed l1_added y_ready a_transposed aT_ready o_summed o_added out_stored
""".split()
SEMAPHORE_RINGS = {"l0_tab": RING, "l0_gathered": RING, "l1_tab": SRING, "l1_gathered": SRING,
                   "G_stored": 2, "G_loaded": SRING, "staged_d": 2, "staged_s": 2, "scattered_d": 2, "scattered_s": 2}
EMPTY = COLS // 2


def gnn_kernel(nc, x, src, dst, kv, W_lin, W_gcn, b_gcn, gamma, beta, Wq, bq, Wk, bk, Wv, bv, Wo, bo, out):
    m = dict(x=x, kv=kv, out=out, keys={"dst": dst, "src": src})
    m["arg"] = {"W_lin": W_lin, "W_gcn": W_gcn, "Wq": Wq, "Wk": Wk, "Wv": Wv, "Wo": Wo, "bq": bq, "bk": bk,
             "b_gcn": b_gcn, "gamma": gamma, "beta": beta, "bv": bv, "bo": bo}
    m["table_d"] = nc.dram_tensor("table_d", (SORTED_AT + NGD * GE + COLS, 2), I32).ap()
    m["table_s"] = nc.dram_tensor("table_s", (NGS * SGE + COLS, 2), I32).ap()
    m["g_dram"] = nc.dram_tensor("g_dram", (NT * P, D), F32).ap()
    m["G_dram"] = nc.dram_tensor("G_dram", (NT * PARTS * P, P + 1), F32).ap()

    with ExitStack() as whole:
        def place(stack, name, shape, dt=F32):
            return stack.enter_context(nc.sbuf_tensor(name, shape, dt))

        for name in SEMAPHORES:
            m[name] = whole.enter_context(nc.semaphore(name))
        for name, n in SEMAPHORE_RINGS.items():
            m[name] = [whole.enter_context(nc.semaphore(f"{name}{i}")) for i in range(n)]
        m["bank"] = [whole.enter_context(nc.psum_tensor(f"bank{i}", [P, 512], F32)) for i in range(8)]

        for name, shape, dt in (
                ("ident", [P, P], F32), ("ones", [P, P], F32), ("iota_n", [P, P], F32), ("iota_h", [P, P], F32), ("headmask", [P, HEADS], F32),
                ("out_b", [P, P], BF16), ("wvo", [P, HEADS * D], F32), ("bvo", [1, D], F32), ("used_i", [P, 1], I32),
                ("wkT", [P, D], F32), ("xres", [P, NT, D], F32), ("mx", [P, STILES], F32), ("hT", [P, 2, P], F32),
                ("tab", [P, RING, GC, 2], I32), ("tab_s", [P, SRING, SGC, 2], I32),
                ("tile_si", [P, NGS], I32), ("node_s", [P, NGS], F32)):
            m[name] = place(whole, name, shape, dt)
        m["w"] = {n: place(whole, f"w_{n}", [P, D if n not in ("bq", "bk", "bv") else 1]) for n in m["arg"]}

        with ExitStack() as front:
            small = ("stat", "mean", "var", "std", "rstd", "deg", "dinv")
            for name, shape, dt in (
                    *((n, [P, NT], F32) for n in small), ("flags", [P, 4], F32), ("flags_i", [P, 1], I32),
                    ("qscale", [P, HEADS], F32), ("qbias", [P, HEADS], F32), ("of_tile", [P, 2], F32), ("steps", [P, P], F32),
                    ("over", [P, COUNTS], F32), ("one_minus_t", [P, COUNTS], F32),
                    ("before", [P, P], F32), ("wvT", [P, D], F32), ("wo_heads", [P, HEADS, D], F32), ("w_linT", [P, D], F32), ("w12", [P, D], F32), ("hs", [P, 2, D], F32),
                    ("iota_d", [P, NGD], F32), ("iota_s", [P, NGS], F32), ("iota_t", [P, STILES], F32), ("minus_t", [P, STILES], F32),
                    ("cnt", [P, 64], F32), ("ng", [P, 64], F32), ("first_d", [P, 64], F32), ("base_d", [P, 64], F32),
                    ("end", [P, 64], F32), ("adj", [P, 64], F32), ("step", [P, 64], F32), ("tot", [P, 64], F32),
                    ("ngi", [P, STILES], I32), ("cnt_s", [P, STILES], F32), ("first_s", [P, STILES], F32),
                    ("end_s", [P, STILES], F32), ("base_s", [P, STILES], F32), ("past", [P, NGS], F32),
                    ("at_f", [P, NGD], F32), ("at_d", [P, NGD], I32), ("tile_d", [P, NGD], F32), ("tile_di", [P, NGD], I32),
                    ("node_d", [P, NGD], F32), ("tile_s", [P, NGS], F32),
                    ("row_st", [P, 2, SC], I32), ("pair_st", [P, 2, SC, 2], I32),
                    ("work", [P, NT, D], F32), ("acc", [P, NT, D], F32),
                    ("tile_of", [P, COLS], F32), ("row", [P, COLS], I32), ("pairs", [P, COLS, 2], I32)):
                m[name] = place(front, name, shape, dt)
            with ExitStack() as sorting:
                for name, shape, dt in (
                        ("square", [P, COLS], F32), ("mask", [P, 2, COLS], F32), ("cum", [P, 2, COLS], F32),
                        ("g_rows", [P, RING, GC, D], F32)):
                    m[name] = place(sorting, name, shape, dt)
                m["raw"] = {k: place(sorting, f"raw_{k}", [P, COLS], I32) for k in ("dst", "src")}
                m["next"] = m["cum"][:, 1, :].bitcast(I32)
                m["empty"] = m["g_rows"][:, :, :, :].rearrange("p u c d -> p (u c d)")[:, 0:2 * EMPTY].bitcast(I32).rearrange("p (j w) -> p j w", w=2)
                m["hot"] = m["work"][:, 0:RING * GC, :].rearrange("p (u c) n -> p u c n", u=RING)
                both = m["mask"][:, :, :].rearrange("p k j -> p (k j)")
                m["hot_p"] = both[:, 0:HC * P].bitcast(BF16).rearrange("p (k c n) -> p k c n", k=2, c=HC)
                m["hot_t"] = both[:, HC * P:HC * (P + NT)].bitcast(BF16).rearrange("p (k c n) -> p k c n", k=2, c=HC)
                first_block(nc, m)
                unsorted_block(nc, m)
                layer0_block(nc, m)
            for name, shape, dt in (("qm", [P, 2, PARTS, HEADS, SN], F32), ("gst", [P, 2, PARTS, P + 1], F32)):
                m[name] = place(front, name, shape, dt)
            nodes_block(nc, m)
        with ExitStack() as back:
            for name, shape, dt in (
                    ("agg", [P, STILES, VW], F32), ("kv_rows", [P, SRING, SGC, D + VW], F32), ("G", [P, SRING, P + 1], F32),
                    ("others", [P, SRING, SGC, P], BF16), ("kT", [P, 2, SGE], F32), ("ex", [P, 2, SGE], F32), ("exT", [P, 2, SGE], F32),
                    ("aT", [P, 2, HEADS, P], F32), ("has", [1, 2, P], F32), ("y", [P, 2, PARTS, VW], F32), ("rl", [P, STILES], F32),
                    *((n, [P, SRING], F32) for n in ("gmax", "mnew", "drop", "shift", "decay"))):
                m[name] = place(back, name, shape, dt)
            layer1_block(nc, m)
            output_block(nc, m)


_VECTORS = {"W_lin": "L0_gnn_W_lin", "W_gcn": "L0_gnn_W_gcn", "b_gcn": "L0_gnn_b_gcn", "gamma": "L0_gnn_gamma",
            "beta": "L0_gnn_beta", "Wq": "L1_gnn_Wq", "bq": "L1_gnn_bq", "Wk": "L1_gnn_Wk", "bk": "L1_gnn_bk",
            "Wv": "L1_gnn_Wv", "bv": "L1_gnn_bv", "Wo": "L1_gnn_Wo", "bo": "L1_gnn_bo"}


def kernel(**inputs):
    import numpy as _np
    import concourse.bacc as _bacc
    from concourse import mybir as _mybir
    from concourse.bass_utils import run_bass_kernel_spmd as _run

    nc = _bacc.Bacc("TRN2", target_bir_lowering=False, num_devices=1)
    host = {"x": inputs["x"], "src": inputs["src"], "dst": inputs["dst"],
            "kv": _np.concatenate([_np.asarray(inputs["edge_attr_128"]), _np.asarray(inputs["edge_attr_128_n2"])], axis=1)}
    host.update({short: inputs[name] for short, name in _VECTORS.items()})
    arrays, args = {}, {}
    for name, value in host.items():
        a = _np.ascontiguousarray(value)
        arrays[f"in_{name}"] = a
        args[name] = nc.dram_tensor(f"in_{name}", a.shape, _mybir.dt.from_np(a.dtype), kind="ExternalInput").ap()
    args["out"] = nc.dram_tensor("out", (N, D), F32, kind="ExternalOutput").ap()
    gnn_kernel(nc, **args)
    r = _run(nc, [arrays], core_ids=[0])
    return r.results[0]["out"]
```
